# Optimizing a Trainium2 kernel written in Bass

```python
import numpy as np
import jax
import jax.numpy as jnp

def _softmax(x, axis=-1):
    return jax.nn.softmax(x, axis=axis)

def _gelu(x):
    return jax.nn.gelu(x, approximate=True)

def _silu(x):
    return jax.nn.silu(x)

def _sigmoid(x):
    return jax.nn.sigmoid(x)

def _layernorm(x, axis=-1, eps=1e-05):
    m = jnp.mean(x, axis=axis, keepdims=True)
    v = jnp.var(x, axis=axis, keepdims=True)
    return (x - m) / jnp.sqrt(v + eps)

def _scatter_add(tgt, idx, src, axis=0):
    return tgt.at[idx].add(src)

def _segment_sum(src, seg, n):
    return jax.ops.segment_sum(src, seg, n)
kernel_name = 'mk_dlrm_tower_d1_rec_r8_269da2'

def setup_inputs(seed: int=0):
    np.random.seed(seed)
    _w = jnp.asarray

    def _rec_inputs():
        import jax
        import jax.numpy as jnp
        _tk = jax.random.key(seed)
        dense_ctx = jax.random.normal(jax.random.fold_in(_tk, 190), (512, 16), jnp.float32)
        ids = jnp.stack([jax.random.randint(jax.random.fold_in(_tk, 200 + f), (512,), 0, v, jnp.int32) for f, v in enumerate([12500, 125000, 125000, 125000, 1250, 12500, 12500, 12500, 1250, 125000, 1000, 1250, 1250, 12500, 12500, 1250, 12500, 1000, 1000, 125000, 1250, 12500, 12500, 12500, 1250, 12500, 1000, 1000, 1000, 12500, 1000, 1250, 1250, 125000, 1000, 1000, 1250, 125000, 1250])], axis=1)
        tbl_0 = 0.05 * jax.random.normal(jax.random.fold_in(_tk, 500 + 0), (12500, 16), jnp.float32)
        tbl_1 = 0.05 * jax.random.normal(jax.random.fold_in(_tk, 500 + 1), (125000, 16), jnp.float32)
        tbl_2 = 0.05 * jax.random.normal(jax.random.fold_in(_tk, 500 + 2), (125000, 16), jnp.float32)
        tbl_3 = 0.05 * jax.random.normal(jax.random.fold_in(_tk, 500 + 3), (125000, 16), jnp.float32)
        tbl_4 = 0.05 * jax.random.normal(jax.random.fold_in(_tk, 500 + 4), (1250, 16), jnp.float32)
        tbl_5 = 0.05 * jax.random.normal(jax.random.fold_in(_tk, 500 + 5), (12500, 16), jnp.float32)
        tbl_6 = 0.05 * jax.random.normal(jax.random.fold_in(_tk, 500 + 6), (12500, 16), jnp.float32)
        tbl_7 = 0.05 * jax.random.normal(jax.random.fold_in(_tk, 500 + 7), (12500, 16), jnp.float32)
        tbl_8 = 0.05 * jax.random.normal(jax.random.fold_in(_tk, 500 + 8), (1250, 16), jnp.float32)
        tbl_9 = 0.05 * jax.random.normal(jax.random.fold_in(_tk, 500 + 9), (125000, 16), jnp.float32)
        tbl_10 = 0.05 * jax.random.normal(jax.random.fold_in(_tk, 500 + 10), (1000, 16), jnp.float32)
        tbl_11 = 0.05 * jax.random.normal(jax.random.fold_in(_tk, 500 + 11), (1250, 16), jnp.float32)
        tbl_12 = 0.05 * jax.random.normal(jax.random.fold_in(_tk, 500 + 12), (1250, 16), jnp.float32)
        tbl_13 = 0.05 * jax.random.normal(jax.random.fold_in(_tk, 500 + 13), (12500, 16), jnp.float32)
        tbl_14 = 0.05 * jax.random.normal(jax.random.fold_in(_tk, 500 + 14), (12500, 16), jnp.float32)
        tbl_15 = 0.05 * jax.random.normal(jax.random.fold_in(_tk, 500 + 15), (1250, 16), jnp.float32)
        tbl_16 = 0.05 * jax.random.normal(jax.random.fold_in(_tk, 500 + 16), (12500, 16), jnp.float32)
        tbl_17 = 0.05 * jax.random.normal(jax.random.fold_in(_tk, 500 + 17), (1000, 16), jnp.float32)
        tbl_18 = 0.05 * jax.random.normal(jax.random.fold_in(_tk, 500 + 18), (1000, 16), jnp.float32)
        tbl_19 = 0.05 * jax.random.normal(jax.random.fold_in(_tk, 500 + 19), (125000, 16), jnp.float32)
        tbl_20 = 0.05 * jax.random.normal(jax.random.fold_in(_tk, 500 + 20), (1250, 16), jnp.float32)
        tbl_21 = 0.05 * jax.random.normal(jax.random.fold_in(_tk, 500 + 21), (12500, 16), jnp.float32)
        tbl_22 = 0.05 * jax.random.normal(jax.random.fold_in(_tk, 500 + 22), (12500, 16), jnp.float32)
        tbl_23 = 0.05 * jax.random.normal(jax.random.fold_in(_tk, 500 + 23), (12500, 16), jnp.float32)
        tbl_24 = 0.05 * jax.random.normal(jax.random.fold_in(_tk, 500 + 24), (1250, 16), jnp.float32)
        tbl_25 = 0.05 * jax.random.normal(jax.random.fold_in(_tk, 500 + 25), (12500, 16), jnp.float32)
        tbl_26 = 0.05 * jax.random.normal(jax.random.fold_in(_tk, 500 + 26), (1000, 16), jnp.float32)
        tbl_27 = 0.05 * jax.random.normal(jax.random.fold_in(_tk, 500 + 27), (1000, 16), jnp.float32)
        tbl_28 = 0.05 * jax.random.normal(jax.random.fold_in(_tk, 500 + 28), (1000, 16), jnp.float32)
        tbl_29 = 0.05 * jax.random.normal(jax.random.fold_in(_tk, 500 + 29), (12500, 16), jnp.float32)
        tbl_30 = 0.05 * jax.random.normal(jax.random.fold_in(_tk, 500 + 30), (1000, 16), jnp.float32)
        tbl_31 = 0.05 * jax.random.normal(jax.random.fold_in(_tk, 500 + 31), (1250, 16), jnp.float32)
        tbl_32 = 0.05 * jax.random.normal(jax.random.fold_in(_tk, 500 + 32), (1250, 16), jnp.float32)
        tbl_33 = 0.05 * jax.random.normal(jax.random.fold_in(_tk, 500 + 33), (125000, 16), jnp.float32)
        tbl_34 = 0.05 * jax.random.normal(jax.random.fold_in(_tk, 500 + 34), (1000, 16), jnp.float32)
        tbl_35 = 0.05 * jax.random.normal(jax.random.fold_in(_tk, 500 + 35), (1000, 16), jnp.float32)
        tbl_36 = 0.05 * jax.random.normal(jax.random.fold_in(_tk, 500 + 36), (1250, 16), jnp.float32)
        tbl_37 = 0.05 * jax.random.normal(jax.random.fold_in(_tk, 500 + 37), (125000, 16), jnp.float32)
        tbl_38 = 0.05 * jax.random.normal(jax.random.fold_in(_tk, 500 + 38), (1250, 16), jnp.float32)
        _rk = jax.random.fold_in(_tk, 7)
        W_top1 = 0.05 * jax.random.normal(jax.random.fold_in(_tk, 801), (400, 512), jnp.float32)
        W_top2 = 0.0441942 * jax.random.normal(jax.random.fold_in(_tk, 802), (512, 256), jnp.float32)
        W_top3 = 0.0625 * jax.random.normal(jax.random.fold_in(_tk, 803), (256, 1), jnp.float32)
        b_top1 = jnp.zeros((512,), jnp.float32)
        b_top2 = jnp.zeros((256,), jnp.float32)
        return (dense_ctx, ids, tbl_0, tbl_1, tbl_2, tbl_3, tbl_4, tbl_5, tbl_6, tbl_7, tbl_8, tbl_9, tbl_10, tbl_11, tbl_12, tbl_13, tbl_14, tbl_15, tbl_16, tbl_17, tbl_18, tbl_19, tbl_20, tbl_21, tbl_22, tbl_23, tbl_24, tbl_25, tbl_26, tbl_27, tbl_28, tbl_29, tbl_30, tbl_31, tbl_32, tbl_33, tbl_34, tbl_35, tbl_36, tbl_37, tbl_38, W_top1, b_top1, W_top2, b_top2, W_top3)
    dense_ctx, ids, tbl_0, tbl_1, tbl_2, tbl_3, tbl_4, tbl_5, tbl_6, tbl_7, tbl_8, tbl_9, tbl_10, tbl_11, tbl_12, tbl_13, tbl_14, tbl_15, tbl_16, tbl_17, tbl_18, tbl_19, tbl_20, tbl_21, tbl_22, tbl_23, tbl_24, tbl_25, tbl_26, tbl_27, tbl_28, tbl_29, tbl_30, tbl_31, tbl_32, tbl_33, tbl_34, tbl_35, tbl_36, tbl_37, tbl_38, W_top1, b_top1, W_top2, b_top2, W_top3 = _rec_inputs()

    def _L0_rec_setup():
        import jax, jax.numpy as jnp
        import numpy as np
        B, F0, D = (256, 39, 16)
        CROSS = [128, 128, 128]
        key = jax.random.key(seed)
        k0, k1, k2, k3 = jax.random.split(key, 4)
        inputs = jax.random.normal(k0, (B, F0, D), dtype=jnp.float32)
        f0 = jax.random.normal(k1, (F0 * F0, CROSS[0]), dtype=jnp.float32) * 0.05
        f1 = jax.random.normal(k2, (CROSS[0] * F0, CROSS[1]), dtype=jnp.float32) * 0.05
        f2 = jax.random.normal(k3, (CROSS[1] * F0, CROSS[2]), dtype=jnp.float32) * 0.05
        return {'inputs': inputs, 'f0': f0, 'f1': f1, 'f2': f2}
    _L0_rec_all = _L0_rec_setup()
    _L0_rec_in = {k: v for k, v in _L0_rec_all.items() if k in ('f0', 'f1', 'f2')}
    del _L0_rec_all
    return {'dense_ctx': dense_ctx, 'ids': ids, 'tbl_0': tbl_0, 'tbl_1': tbl_1, 'tbl_2': tbl_2, 'tbl_3': tbl_3, 'tbl_4': tbl_4, 'tbl_5': tbl_5, 'tbl_6': tbl_6, 'tbl_7': tbl_7, 'tbl_8': tbl_8, 'tbl_9': tbl_9, 'tbl_10': tbl_10, 'tbl_11': tbl_11, 'tbl_12': tbl_12, 'tbl_13': tbl_13, 'tbl_14': tbl_14, 'tbl_15': tbl_15, 'tbl_16': tbl_16, 'tbl_17': tbl_17, 'tbl_18': tbl_18, 'tbl_19': tbl_19, 'tbl_20': tbl_20, 'tbl_21': tbl_21, 'tbl_22': tbl_22, 'tbl_23': tbl_23, 'tbl_24': tbl_24, 'tbl_25': tbl_25, 'tbl_26': tbl_26, 'tbl_27': tbl_27, 'tbl_28': tbl_28, 'tbl_29': tbl_29, 'tbl_30': tbl_30, 'tbl_31': tbl_31, 'tbl_32': tbl_32, 'tbl_33': tbl_33, 'tbl_34': tbl_34, 'tbl_35': tbl_35, 'tbl_36': tbl_36, 'tbl_37': tbl_37, 'tbl_38': tbl_38, 'W_top1': W_top1, 'b_top1': b_top1, 'W_top2': W_top2, 'b_top2': b_top2, 'W_top3': W_top3, 'L0_rec_f0': _L0_rec_in['f0'], 'L0_rec_f1': _L0_rec_in['f1'], 'L0_rec_f2': _L0_rec_in['f2']}

def reference(dense_ctx, ids, tbl_0, tbl_1, tbl_2, tbl_3, tbl_4, tbl_5, tbl_6, tbl_7, tbl_8, tbl_9, tbl_10, tbl_11, tbl_12, tbl_13, tbl_14, tbl_15, tbl_16, tbl_17, tbl_18, tbl_19, tbl_20, tbl_21, tbl_22, tbl_23, tbl_24, tbl_25, tbl_26, tbl_27, tbl_28, tbl_29, tbl_30, tbl_31, tbl_32, tbl_33, tbl_34, tbl_35, tbl_36, tbl_37, tbl_38, W_top1, b_top1, W_top2, b_top2, W_top3, L0_rec_f0, L0_rec_f1, L0_rec_f2):
    import jax
    import jax.numpy as jnp

    def _L0_rec_ref(inputs, f0, f1, f2):
        import jax, jax.numpy as jnp
        import numpy as np
        B, F0, D = (256, 39, 16)
        CROSS = [128, 128, 128]
        filters = [f0, f1, f2]
        x0 = inputs
        xk = inputs
        outs = []
        for W in filters:
            b, f, d = x0.shape
            g = xk.shape[1]
            z = jnp.einsum('bfd,bgd->bfgd', x0, xk).reshape(b, f * g, d)
            cur = jnp.einsum('bpd,pm->bmd', z, W)
            outs.append(cur)
            xk = cur
        result = jnp.concatenate(outs, axis=1)
        return jnp.sum(result, axis=-1)
    e = jnp.stack([tbl_0[ids[:, 0]], tbl_1[ids[:, 1]], tbl_2[ids[:, 2]], tbl_3[ids[:, 3]], tbl_4[ids[:, 4]], tbl_5[ids[:, 5]], tbl_6[ids[:, 6]], tbl_7[ids[:, 7]], tbl_8[ids[:, 8]], tbl_9[ids[:, 9]], tbl_10[ids[:, 10]], tbl_11[ids[:, 11]], tbl_12[ids[:, 12]], tbl_13[ids[:, 13]], tbl_14[ids[:, 14]], tbl_15[ids[:, 15]], tbl_16[ids[:, 16]], tbl_17[ids[:, 17]], tbl_18[ids[:, 18]], tbl_19[ids[:, 19]], tbl_20[ids[:, 20]], tbl_21[ids[:, 21]], tbl_22[ids[:, 22]], tbl_23[ids[:, 23]], tbl_24[ids[:, 24]], tbl_25[ids[:, 25]], tbl_26[ids[:, 26]], tbl_27[ids[:, 27]], tbl_28[ids[:, 28]], tbl_29[ids[:, 29]], tbl_30[ids[:, 30]], tbl_31[ids[:, 31]], tbl_32[ids[:, 32]], tbl_33[ids[:, 33]], tbl_34[ids[:, 34]], tbl_35[ids[:, 35]], tbl_36[ids[:, 36]], tbl_37[ids[:, 37]], tbl_38[ids[:, 38]]], axis=1)
    z = _L0_rec_ref(e, L0_rec_f0, L0_rec_f1, L0_rec_f2)
    z = z.reshape(z.shape[0], -1)
    h = jnp.concatenate([z, dense_ctx], axis=1)
    h = jnp.maximum(h @ W_top1 + b_top1, 0.0)
    h = jnp.maximum(h @ W_top2 + b_top2, 0.0)
    y = h @ W_top3
    return y

_drawn_inputs = setup_inputs


def setup_inputs(seed=0):
    import zlib

    import numpy as np

    out = dict(_drawn_inputs(seed))
    spreads = {'b_top1': (0.0, 0.671), 'b_top2': (0.0, 0.301)}
    factors = {'tbl_0': 4.583,
     'tbl_1': 4.976,
     'tbl_2': 5.033,
     'tbl_3': 4.994,
     'tbl_4': 4.666,
     'tbl_5': 5.174,
     'tbl_6': 4.84,
     'tbl_7': 4.661,
     'tbl_8': 4.897,
     'tbl_9': 4.291,
     'tbl_10': 5.447,
     'tbl_11': 4.551,
     'tbl_12': 4.697,
     'tbl_13': 4.578,
     'tbl_14': 4.909,
     'tbl_15': 5.197,
     'tbl_16': 5.602,
     'tbl_17': 4.91,
     'tbl_18': 5.197,
     'tbl_19': 4.785,
     'tbl_20': 4.899,
     'tbl_21': 4.981,
     'tbl_22': 4.548,
     'tbl_23': 4.634,
     'tbl_24': 4.348,
     'tbl_25': 4.385,
     'tbl_26': 4.674,
     'tbl_27': 5.091,
     'tbl_28': 4.852,
     'tbl_29': 4.753,
     'tbl_30': 5.076,
     'tbl_31': 4.392,
     'tbl_32': 4.746,
     'tbl_33': 5.199,
     'tbl_34': 4.915,
     'tbl_35': 4.753,
     'tbl_36': 4.959,
     'tbl_37': 4.94,
     'tbl_38': 5.031,
     'L0_rec_f1': 5.387,
     'L0_rec_f2': 8.0}
    for name, (base, spread) in spreads.items():
        noise = np.random.default_rng([zlib.crc32(name.encode()), seed]).standard_normal(out[name].shape)
        drawn = base * np.exp(spread * noise) if base else spread * noise
        out[name] = jnp.asarray(drawn.astype(out[name].dtype))
    for name, factor in factors.items():
        out[name] = (out[name] * factor).astype(out[name].dtype)
    return out
```

```python
from contextlib import ExitStack

import concourse.bass as bass
from concourse import mybir

F32 = mybir.dt.float32
F32R = mybir.dt.float32r
I32 = mybir.dt.int32
ALU = mybir.AluOpType
ACT = mybir.ActivationFunctionType
AX_X = mybir.AxisListType.X

P = 128
NF = 39
D = 16
M = 128
NB = 512
NCHUNK = NB // P
GROUPS = 4
TILES = 4
BT = P // D
BG = BT * TILES
COLS = BG * D
TPC = GROUPS * TILES

NK = NF // 2 + 1
KB = 3
ZB = -(-NK // KB)
XW = NF + NK - 1

FB = 4
KIND = "DADDADADAD"
NBANK = len(KIND)
SLOTS = TILES * NBANK
WIDTH = [min(FB, NF - FB * j) for j in range(NBANK)]
YB = 4
STT = sum(w for w, k in zip(WIDTH, KIND) if k == "D")
MUL = sum(w for w, k in zip(WIDTH, KIND) if k == "A")
NA = KIND.count("A")
ADDS = NA

PROD0, STEP = 8, 3
TRANS0 = PROD0 + 3
L1_LAG = 5
CUR_SLOT = TRANS0 + STEP * (ZB - 1) + L1_LAG + 1
GRAM = 8
GATHERS = 4

H1, H2 = 512, 256
N1, N2 = H1 // P, H2 // P
ND = 16


def stt_count(tile, j):
    return tile * STT + sum(w for w, k in zip(WIDTH[:j + 1], KIND) if k == "D")


def mul_count(tile, j):
    return tile * MUL + sum(w for w, k in zip(WIDTH[:j + 1], KIND) if k == "A")


def krows(k):
    return NF * min(KB, NK - KB * k)


def build(nc, dense_ctx, ids, tables, w_top1, b_top1, w_top2, b_top2, w_top3, f0, f1, f2,
          identity, sample_mask, out):
    with ExitStack() as ctx:
        def sb(name, shape, dt=F32):
            return ctx.enter_context(nc.sbuf_tensor(name, shape, dt))

        def psum(name, shape):
            return ctx.enter_context(nc.psum_tensor(name, shape, F32))

        def sem(name):
            return ctx.enter_context(nc.semaphore(name))

        ident = sb("ident", [P, P])
        mask = sb("mask", [P, BT])
        ids_sb = sb("ids_sb", [P, NF], I32)
        xg = sb("xg", [P, NF, D])
        xt = sb("xt", [NF, P * D])
        xs = sb("xs", [P, GROUPS, TILES, XW])
        zp = sb("zp", [P, 3, TILES, KB * NF])
        z_hi = sb("z_hi", [P, 3, COLS], F32R)
        z_lo = sb("z_lo", [P, 3, COLS], F32R)
        wa = sb("wa", [P, ZB, M])
        wb = sb("wb", [P, ZB, M])
        ws = sb("ws", [P, ZB, M])
        ws_hi = sb("ws_hi", [P, ZB, M], F32R)
        ws_lo = sb("ws_lo", [P, ZB, M], F32R)
        w1 = sb("w1", [P, NF * M])
        w1_hi = sb("w1_hi", [P, NF * M], F32R)
        w1_lo = sb("w1_lo", [P, NF * M], F32R)
        w2 = sb("w2", [P, NF, M])
        c_hi = sb("c_hi", [P, 2, COLS], F32R)
        c_lo = sb("c_lo", [P, 2, COLS], F32R)
        scaled = sb("scaled", [P, 2, NA, FB * M])
        psumg = sb("psumg", [P, 2, FB * M])
        part = sb("part", [P, 2, 4, M])
        half = sb("half", [P, 2, 2, M])
        cur2 = sb("cur2", [P, 2, M])
        xd = sb("xd", [P, 2, BT, NF + 1])
        gs = sb("gs", [P, NF + 1, P])
        z1 = sb("z1", [P, P])
        z1m = sb("z1m", [P, P])
        z2m = sb("z2m", [P, P])
        z3m = sb("z3m", [P, P])
        wt1 = sb("wt1", [P, 3, H1])
        wt1d = sb("wt1d", [ND, H1])
        wt2 = sb("wt2", [P, N1, H2])
        wt3 = sb("wt3", [P, N2])
        b1 = sb("b1", [P, N1])
        b2 = sb("b2", [P, N2])
        dn = sb("dn", [P, NCHUNK, ND])
        dnt = sb("dnt", [ND, NB])
        h1s = sb("h1s", [P, N1, P])
        h2s = sb("h2s", [P, N2, P])
        ysb = sb("ysb", [1, NB])

        y_ps = psum("y_ps", [P, YB, FB * M])
        t_ps = psum("t_ps", [P, 2, COLS])
        c_ps = psum("c_ps", [P, COLS])
        m_ps = psum("m_ps", [P, COLS])

        ident_in = sem("ident_in")
        pairs_in = sem("pairs_in")
        pairs_zero = sem("pairs_zero")
        w1_in = sem("w1_in")
        w2_in = sem("w2_in")
        top_in = sem("top_in")
        dense_in = sem("dense_in")
        ids_in = sem("ids_in")
        gathered = sem("gathered")
        ones_set = sem("ones_set")
        ws_sum = sem("ws_sum")
        ws_high = sem("ws_high")
        ws_low = sem("ws_low")
        w1_high = sem("w1_high")
        w1_low = sem("w1_low")
        turned = sem("turned")
        turned_out = sem("turned_out")
        multiplied = sem("multiplied")
        z_turned = sem("z_turned")
        z_high = sem("z_high")
        z_low = sem("z_low")
        l1_step = sem("l1_step")
        c_high = sem("c_high")
        c_low = sem("c_low")
        z1_sum = sem("z1_sum")
        z1_kept = sem("z1_kept")
        y_ready = sem("y_ready")
        stt_done = sem("stt_done")
        mul_done = sem("mul_done")
        add_done = sem("add_done")
        half_done = sem("half_done")
        cur2_ready = sem("cur2_ready")
        xd_ready = sem("xd_ready")
        gram_ready = sem("gram_ready")
        gram_out = sem("gram_out")
        z2_kept = sem("z2_kept")
        tail_ready = sem("tail_ready")
        tail_out = sem("tail_out")
        y_out = sem("y_out")

        def wait(eng, s, n):
            if not isinstance(n, int) or n > 0:
                eng.wait_ge(s, n)

        def turn1_count(chunk, piece):
            return chunk * 8 + 1 + piece + 1

        def turn2_count(chunk, q):
            return chunk * 8 + 5 + q + 1

        ids_rows = ids.rearrange("(c p) f -> c p f", p=P)
        out_rows = out.rearrange("(c b) o -> c (o b)", b=P)

        def pair_loads():
            flat = f0
            for k in range(NK):
                kb, r0 = divmod(k, KB)
                r0 *= NF
                for lo, hi in ((0, NF - k), (NF - k, NF)):
                    if hi <= lo:
                        continue
                    first = lo * NF + (lo + k) % NF
                    a = flat[first:first + (hi - lo - 1) * (NF + 1) + 1:NF + 1, :]
                    yield wa[r0 + lo:r0 + hi, kb, :], a
                    if k:
                        first = ((lo + k) % NF) * NF + lo
                        b = flat[first:first + (hi - lo - 1) * (NF + 1) + 1:NF + 1, :]
                        yield wb[r0 + lo:r0 + hi, kb, :], b

        pair_list = list(pair_loads())

        block = ctx.enter_context(nc.Block())

        @block.sync
        def _(sp):
            def load_ids(chunk):
                sp.dma_start(ids_sb[:], ids_rows[chunk]).then_inc(ids_in, 16)

            def send(chunk):
                sp.wait_ge(tail_out, 4 * chunk + 4)
                sp.dma_start(out_rows[chunk:chunk + 1], ysb[:, chunk * P:(chunk + 1) * P]).then_inc(y_out, 16)

            load_ids(0)
            sp.dma_start(ident[:], identity).then_inc(ident_in, 16)
            sp.dma_start(mask[:], sample_mask).then_inc(ident_in, 16)
            sp.dma_start(w1[:].rearrange("g (f m) -> g f m", m=M),
                         f1.rearrange("(f g) m -> g f m", g=P)).then_inc(w1_in, 16)
            sp.wait_ge(pairs_zero, 1)
            for to, of in pair_list[0::2]:
                sp.dma_start(to, of).then_inc(pairs_in, 16)
            sp.dma_start(w2[:], f2.rearrange("(f g) m -> g f m", g=P)).then_inc(w2_in, 16)
            sp.wait_ge(gathered, 16 * NF)
            load_ids(1)

            for c in range(2, NCHUNK):
                sp.wait_ge(gathered, 16 * NF * c)
                load_ids(c)
                send(c - 2)
            send(NCHUNK - 2)
            send(NCHUNK - 1)
            sp.wait_ge(y_out, 16 * NCHUNK)

        @block.gpsimd
        def _(pool):
            def gather(feats):
                for f in feats:
                    nc.gpsimd.indirect_dma_start(
                        xg[:, f, :], None, tables[f],
                        bass.IndirectOffsetOnAxis(ap=ids_sb[:, f:f + 1], axis=0)).then_inc(gathered, 16)

            nc.gpsimd.memset(wb[:], 0.0).then_inc(pairs_zero, 1)
            pool.wait_ge(ids_in, 16)
            gather(range(NF))
            pool.wait_ge(ident_in, 32)
            for u in range(2):
                nc.gpsimd.tensor_copy(xd[:, u, :, NF], mask[:]).then_inc(ones_set, 1)
            pool.wait_ge(ones_set, 2)

            def chunk(c, first=False, last=False):
                for q in range(GROUPS):
                    for t in range(TILES):
                        tile = c * TPC + q * TILES + t
                        u = t % 2
                        if t == 0:
                            pool.wait_ge(turned_out, turn2_count(c, q))
                        wait(pool, gram_ready, tile - 1)
                        nc.gpsimd.tensor_tensor(
                            xd[:, u, :, 0:NF],
                            mask[:].unsqueeze(2).to_broadcast([P, BT, NF]),
                            xs[:, q, t, 0:NF].unsqueeze(1).to_broadcast([P, BT, NF]),
                            ALU.mult).then_inc(xd_ready, 1)
                        for a in range(1, NA):
                            pool.wait_ge(mul_done, tile * MUL + FB * (a + 1))
                            wait(pool, add_done, tile * ADDS + a - 1)
                            prev = scaled[:, u, 0, :] if a == 1 else psumg[:, (a - 1) % 2, :]
                            nc.gpsimd.tensor_tensor(psumg[:, a % 2, :], prev, scaled[:, u, a, :],
                                                    ALU.add).then_inc(add_done, 1)
                        pool.wait_ge(add_done, tile * ADDS + NA - 1)
                        wait(pool, cur2_ready, tile - 1)
                        if q == 0 and t == 0 and not last:
                            pool.wait_ge(ids_in, 16 * (c + 2))
                            pool.wait_ge(turned, turn1_count(c, 3))
                        g = psumg[:, (NA - 1) % 2, :].rearrange("p (h m) -> p h m", m=2 * M)
                        nc.gpsimd.tensor_tensor(
                            part[:, u, 2:4, :].rearrange("p h m -> p (h m)"),
                            g[:, 0, :], g[:, 1, :], ALU.add).then_inc(add_done, 1)
                        lo = GATHERS * (q * TILES + t)
                        if lo < NF and not last:
                            gather(range(lo, min(lo + GATHERS, NF)))

            chunk(0, first=True)
            with pool.Fori(1, NCHUNK - 1) as c:
                chunk(c)
            chunk(NCHUNK - 1, last=True)

        @block.scalar
        def _(act):
            def turned_dense():
                act.wait_ge(turned, 1)
                nc.scalar.copy(dnt[:], t_ps[0:ND, 0, :]).then_inc(turned_out, 1)

            def turn1_out(chunk, piece, bank):
                act.wait_ge(turned, turn1_count(chunk, piece))
                to = xt[:].rearrange("f (b d) -> f d b", d=D)[:, 4 * piece:4 * piece + 4, :]
                nc.scalar.copy(to, t_ps[0:NF, bank, :].rearrange("f (d b) -> f d b", b=P)
                               ).then_inc(turned_out, 1)

            def turn2_out(chunk, q, bank):
                act.wait_ge(turned, turn2_count(chunk, q))
                of = t_ps[:, bank, 0:TILES * NF].rearrange("p (t f) -> p t f", f=NF)
                nc.scalar.copy(xs[:, q, :, 0:NF], of)
                nc.scalar.copy(xs[:, q, :, NF:XW], of[:, :, 0:XW - NF]).then_inc(turned_out, 1)

            def z_high_out(g, k, bank):
                act.wait_ge(z_turned, g * ZB + k + 1)
                wait(act, l1_step, g * ZB + k - 2 if k >= 3 else g * ZB)
                nc.scalar.copy(z_hi[0:krows(k), k % 3, :], t_ps[0:krows(k), bank, :]
                               ).then_inc(z_high, 1)

            def c_high_out(g, u):
                act.wait_ge(l1_step, (g + 1) * ZB)
                nc.scalar.copy(c_hi[:, u, :], c_ps[:]).then_inc(c_high, 1)

            def keep_z1(c):
                act.wait_ge(z1_sum, GROUPS * (c + 1))
                nc.scalar.copy(z1m[:], z1[:]).then_inc(z1_kept, 1)

            def gram_read(tile, b0):
                act.wait_ge(gram_ready, tile + 1)
                nc.scalar.copy(gs[:, :, b0:b0 + BT],
                               m_ps[:, 0:BT * (NF + 1)].rearrange("p (b f) -> p f b", f=NF + 1)
                               ).then_inc(gram_out, 1)

            def keep_z2(c):
                act.wait_ge(gram_out, TPC * (c + 1))
                nc.scalar.copy(z2m[:], gs[:, NF, :]).then_inc(z2_kept, 1)

            def z3_out(c):
                act.wait_ge(tail_ready, 4 * c + 1)
                nc.scalar.copy(z3m[:], m_ps[:, 0:P]).then_inc(tail_out, 1)

            def h1_out(c):
                act.wait_ge(tail_ready, 4 * c + 2)
                for n in range(N1):
                    last = nc.scalar.activation(h1s[:, n, :], m_ps[:, n * P:(n + 1) * P], ACT.Relu,
                                                bias=b1[:, n:n + 1])
                last.then_inc(tail_out, 1)

            def h2_out(c):
                act.wait_ge(tail_ready, 4 * c + 3)
                for n in range(N2):
                    last = nc.scalar.activation(h2s[:, n, :], m_ps[:, n * P:(n + 1) * P], ACT.Relu,
                                                bias=b2[:, n:n + 1])
                last.then_inc(tail_out, 1)

            def y_read(c):
                act.wait_ge(tail_ready, 4 * c + 4)
                nc.scalar.copy(ysb[:, bass.ds(c * P, P)], m_ps[0:1, 0:P]).then_inc(tail_out, 1)

            def multiply(tile, q, t, j):
                a = KIND[:j].count("A")
                act.wait_ge(y_ready, tile * NBANK + j + 1)
                wait(act, add_done, (tile - 2) * ADDS + max(a, 1))
                for i in range(FB):
                    f = FB * j + i
                    nc.scalar.activation(
                        scaled[:, t % 2, a, i * M:(i + 1) * M],
                        y_ps[:, (t * NBANK + j) % YB, i * M:(i + 1) * M], ACT.Copy,
                        scale=xs[:, q, t, f:f + 1]).then_inc(mul_done, 1)

            for to, of in pair_list[1::2]:
                if to is pair_list[1][0]:
                    act.wait_ge(pairs_zero, 1)
                act.dma_start(to, of).then_inc(pairs_in, 16)
            act.dma_start(dn[:], dense_ctx.rearrange("(c p) n -> p c n", p=P)).then_inc(dense_in, 16)
            act.dma_start(wt1[:], w_top1[0:3 * M, :].rearrange("(k p) n -> p k n", p=P)).then_inc(top_in, 16)
            act.dma_start(wt1d[:], w_top1[3 * M:3 * M + ND, :]).then_inc(top_in, 16)
            act.dma_start(wt2[:], w_top2.rearrange("(k p) n -> p k n", p=P)).then_inc(top_in, 16)
            act.dma_start(wt3[:], w_top3).then_inc(top_in, 16)
            act.dma_start(b1[:], b_top1).then_inc(top_in, 16)
            act.dma_start(b2[:], b_top2).then_inc(top_in, 16)
            act.wait_ge(w1_in, 16)
            nc.scalar.copy(w1_hi[:], w1[:]).then_inc(w1_high, 1)
            act.wait_ge(ws_sum, 1)
            for k in range(ZB):
                nc.scalar.copy(ws_hi[0:krows(k), k, :], ws[0:krows(k), k, :]).then_inc(ws_high, 1)
            turned_dense()
            for piece in range(4):
                turn1_out(0, piece, (1 + piece) % 2)
            turn2_out(0, 0, 5 % 2)
            for k in range(ZB):
                z_high_out(0, k, (6 + k) % 2)
            c_high_out(0, 0)
            act.wait_ge(top_in, 96)

            def chunk(c, first=False, last=False):
                bank = 13
                for q in range(GROUPS):
                    prep = not (last and q == GROUPS - 1)
                    g1 = c * GROUPS + q + 1
                    for s in range(SLOTS):
                        t, j = divmod(s, NBANK)
                        tile = c * TPC + q * TILES + t
                        if q == GROUPS - 1 and s == 0:
                            keep_z1(c)
                        if KIND[j] == "A":
                            multiply(tile, q, t, j)
                        if prep:
                            if q < 3 and s == 1:
                                turn2_out(c, q + 1, bank % 2)
                                bank += 1
                            if q == 3 and 1 <= s <= 4:
                                turn1_out(c + 1, s - 1, bank % 2)
                                bank += 1
                            if q == 3 and s == 7:
                                turn2_out(c + 1, 0, bank % 2)
                                bank += 1
                            k, r = divmod(s - TRANS0 - 1, STEP)
                            if r == 0 and 0 <= k < ZB:
                                z_high_out(g1, k, bank % 2)
                                bank += 1
                            if s == CUR_SLOT:
                                c_high_out(g1, (q + 1) % 2)
                        if j == GRAM + 1 and not (first and q == 0 and t == 0):
                            gram_read(tile - 1, (q * BG + t * BT - BT) % P)
                        if not first:
                            if q == 0 and s == GRAM + 1:
                                keep_z2(c - 1)
                            if q == 0 and s == 17:
                                z3_out(c - 1)
                            if q == 0 and s == 25:
                                h1_out(c - 1)
                            if q == 0 and s == 33:
                                h2_out(c - 1)
                            if q == 1 and s == 2:
                                y_read(c - 1)

            chunk(0, first=True)
            with act.Fori(1, NCHUNK - 1) as c:
                chunk(c)
            c = NCHUNK - 1
            chunk(c, last=True)
            gram_read(NCHUNK * TPC - 1, P - BT)
            keep_z2(c)
            z3_out(c)
            h1_out(c)
            h2_out(c)
            y_read(c)

        @block.vector
        def _(dve):
            def products(g, k, q):
                if k == 0:
                    dve.wait_ge(turned_out, turn2_count(*q))
                wait(dve, z_turned, g * ZB + k - 2 if k >= 3 else g * ZB)
                nk = min(KB, NK - KB * k)
                w = xs[:, q[1], :, KB * k:KB * k + nk + NF - 1]
                ahead = bass.AP(tensor=w.tensor, offset=w.offset,
                                ap=[w.ap[0], w.ap[1], [1, nk], [1, NF]])
                of = xs[:, q[1], :, 0:NF].unsqueeze(2).to_broadcast([P, TILES, nk, NF])
                to = zp[:, k % 3, :, 0:nk * NF].rearrange("p t (k f) -> p t k f", f=NF)
                nc.vector.tensor_tensor(to, of, ahead, ALU.mult).then_inc(multiplied, 1)

            def z_low_out(g, k, bank):
                dve.wait_ge(z_high, g * ZB + k + 1)
                r = krows(k)
                nc.vector.tensor_tensor(z_lo[0:r, k % 3, :], t_ps[0:r, bank, :],
                                        z_hi[0:r, k % 3, :].bitcast(F32), ALU.subtract).then_inc(z_low, 1)

            def c_low_out(g, u):
                dve.wait_ge(c_high, g + 1)
                nc.vector.tensor_tensor(c_lo[:, u, :], c_ps[:], c_hi[:, u, :].bitcast(F32),
                                        ALU.subtract).then_inc(c_low, 1)

            def z1_out(g, q, kept):
                dve.wait_ge(l1_step, (g + 1) * ZB)
                wait(dve, z1_kept, kept)
                nc.vector.tensor_reduce(z1[:, q * BG:(q + 1) * BG],
                                        c_ps[:].rearrange("m (b d) -> m b d", d=D), AX_X,
                                        ALU.add).then_inc(z1_sum, 1)

            def accumulate(tile, q, t, j):
                dve.wait_ge(y_ready, tile * NBANK + j + 1)
                done = stt_count(0, j) - WIDTH[j]
                for i in range(WIDTH[j]):
                    n = done + i
                    f = FB * j + i
                    y = y_ps[:, (t * NBANK + j) % YB, i * M:(i + 1) * M]
                    to = part[:, t % 2, n % 2, :]
                    x = xs[:, q, t, f:f + 1]
                    if n < 2:
                        wait(dve, half_done, tile - 1)
                        nc.vector.tensor_scalar(to, y, x, None, ALU.mult).then_inc(stt_done, 1)
                    else:
                        dve.wait_ge(stt_done, tile * STT + n - 1)
                        nc.vector.scalar_tensor_tensor(out=to, in0=y, scalar=x, in1=to, op0=ALU.mult,
                                                       op1=ALU.add).then_inc(stt_done, 1)

            def finish(tile, u):
                dve.wait_ge(stt_done, (tile + 1) * STT)
                dve.wait_ge(add_done, (tile + 1) * ADDS)
                nc.vector.tensor_tensor(half[:, u, :, :], part[:, u, 0:2, :], part[:, u, 2:4, :],
                                        ALU.add).then_inc(half_done, 1)
                dve.wait_ge(half_done, tile + 1)
                wait(dve, gram_ready, tile - 1)
                nc.vector.tensor_tensor(cur2[:, u, :], half[:, u, 0, :], half[:, u, 1, :],
                                        ALU.add).then_inc(cur2_ready, 1)

            dve.wait_ge(pairs_in, 16 * len(pair_list))
            for k in range(ZB):
                last = nc.vector.tensor_tensor(ws[0:krows(k), k, :], wa[0:krows(k), k, :],
                                               wb[0:krows(k), k, :], ALU.add)
            last.then_inc(ws_sum, 1)
            for k in range(ZB):
                dve.wait_ge(ws_high, k + 1)
                nc.vector.tensor_tensor(ws_lo[0:krows(k), k, :], ws[0:krows(k), k, :],
                                        ws_hi[0:krows(k), k, :].bitcast(F32), ALU.subtract).then_inc(ws_low, 1)
            dve.wait_ge(w1_high, 1)
            nc.vector.tensor_tensor(w1_lo[:], w1[:], w1_hi[:].bitcast(F32), ALU.subtract).then_inc(w1_low, 1)
            for k in range(ZB):
                products(0, k, (0, 0))
                if k:
                    z_low_out(0, k - 1, (6 + k - 1) % 2)
            z_low_out(0, ZB - 1, (6 + ZB - 1) % 2)
            c_low_out(0, 0)
            z1_out(0, 0, 0)

            def chunk(c, first=False, last=False):
                bank = 13
                for q in range(GROUPS):
                    prep = not (last and q == GROUPS - 1)
                    g1 = c * GROUPS + q + 1
                    nxt = (c, q + 1) if q < 3 else (c + 1, 0)
                    if prep:
                        bank += 5 if q == 3 else 1
                    for s in range(SLOTS):
                        t, j = divmod(s, NBANK)
                        tile = c * TPC + q * TILES + t
                        if KIND[j] == "D":
                            accumulate(tile, q, t, j)
                        if prep:
                            k, r = divmod(s - PROD0, STEP)
                            if r == 0 and 0 <= k < ZB:
                                products(g1, k, nxt)
                            k, r = divmod(s - TRANS0 - 2, STEP)
                            if r == 0 and 0 <= k < ZB:
                                z_low_out(g1, k, bank % 2)
                                bank += 1
                            if s == CUR_SLOT + 1:
                                c_low_out(g1, (q + 1) % 2)
                            if s == CUR_SLOT + 2:
                                z1_out(g1, nxt[1], c + 1 if q == 3 else (c if not first else 0))
                        if j == 4 and not (first and q == 0 and t == 0):
                            finish(tile - 1, (t + 1) % 2)

            chunk(0, first=True)
            with dve.Fori(1, NCHUNK - 1) as c:
                chunk(c)
            chunk(NCHUNK - 1, last=True)
            finish(NCHUNK * TPC - 1, 1)

        @block.tensor
        def _(pe):
            def bank_free(g, k):
                if k < 0:
                    g, k = g - 1, k + ZB
                wait(pe, z_low, g * ZB + k + 1)

            def turn_dense():
                pe.wait_ge(dense_in, 16)
                pe.wait_ge(ident_in, 32)
                for c in range(NCHUNK):
                    last = nc.tensor.transpose(t_ps[0:ND, 0, c * P:(c + 1) * P], dn[:, c, :], ident[:])
                last.then_inc(turned, 1)

            def turn1_waits(chunk, piece, g):
                if piece == 0:
                    pe.wait_ge(gathered, 16 * NF * (chunk + 1))
                if piece < 2:
                    bank_free(g, piece - 2)
                else:
                    pe.wait_ge(turned_out, turn1_count(chunk, piece - 2))

            def turn2_waits(chunk, q, g):
                pe.wait_ge(turned_out, turn1_count(chunk, 3))
                bank_free(g, -2)

            def turn1(piece, bank):
                for i in range(4):
                    d = 4 * piece + i
                    last = nc.tensor.transpose(t_ps[0:NF, bank, i * P:(i + 1) * P], xg[:, :, d], ident[:])
                last.then_inc(turned, 1)

            def turn2(q, bank):
                for t in range(TILES):
                    a = (q * TILES + t) * P
                    last = nc.tensor.transpose(t_ps[:, bank, t * NF:(t + 1) * NF], xt[:, a:a + P],
                                               ident[0:NF, 0:NF])
                last.then_inc(turned, 1)

            def z_turn(g, k, bank, after):
                pe.wait_ge(multiplied, g * ZB + k + 1)
                after()
                r = krows(k)
                for t in range(TILES):
                    last = nc.tensor.transpose(t_ps[0:r, bank, t * P:(t + 1) * P], zp[:, k % 3, t, 0:r],
                                               ident[:])
                last.then_inc(z_turned, 1)

            def layer1(g, k):
                if k == 0:
                    wait(pe, z1_sum, g)
                    wait(pe, c_low, g)
                r = krows(k)
                pe.wait_ge(z_high, g * ZB + k + 1)
                nc.tensor.matmul(c_ps[:], ws_hi[0:r, k, :], z_hi[0:r, k % 3, :], start=(k == 0), stop=False)
                nc.tensor.matmul(c_ps[:], ws_lo[0:r, k, :], z_hi[0:r, k % 3, :], start=False, stop=False)
                pe.wait_ge(z_low, g * ZB + k + 1)
                nc.tensor.matmul(c_ps[:], ws_hi[0:r, k, :], z_lo[0:r, k % 3, :], start=False,
                                 stop=(k == ZB - 1)).then_inc(l1_step, 1)

            def layer2(tile, q, t, j, g, others=lambda: None):
                u = q % 2
                if t == 0 and j == 0:
                    pe.wait_ge(c_high, g)
                    pe.wait_ge(c_low, g)
                pj, pt = j - YB, tile
                if pj < 0:
                    pj, pt = pj + NBANK, tile - 1
                if KIND[pj] == "D":
                    wait(pe, stt_done, stt_count(pt, pj))
                else:
                    wait(pe, mul_done, mul_count(pt, pj))
                n = WIDTH[j] * M
                w = slice(FB * j * M, FB * j * M + n)
                to = y_ps[:, (t * NBANK + j) % YB, 0:n]
                hi = c_hi[:, u, t * P:(t + 1) * P]
                lo = c_lo[:, u, t * P:(t + 1) * P]
                nc.tensor.matmul(to, hi, w1_hi[:, w], start=True, stop=False)
                nc.tensor.matmul(to, hi, w1_lo[:, w], start=False, stop=False)
                others()
                nc.tensor.matmul(to, lo, w1_hi[:, w], start=False, stop=True).then_inc(y_ready, 1)

            def gram(tile, u, tails):
                pe.wait_ge(cur2_ready, tile + 1)
                pe.wait_ge(xd_ready, tile + 1)
                wait(pe, gram_out, tile)
                if tails is not None:
                    pe.wait_ge(tail_out, tails)
                nc.tensor.matmul(m_ps[:, 0:BT * (NF + 1)], cur2[:, u, :],
                                 xd[:, u, :, :].rearrange("p b f -> p (b f)"), start=True,
                                 stop=True).then_inc(gram_ready, 1)

            def layer3(c, lo, hi):
                if lo == 0:
                    pe.wait_ge(gram_out, TPC * (c + 1))
                for f in range(lo, min(hi, NF)):
                    last = nc.tensor.matmul(m_ps[:, 0:P], w2[:, f, :], gs[:, f, :], start=(f == 0),
                                            stop=(f == NF - 1))
                if hi >= NF:
                    last.then_inc(tail_ready, 1)

            def tower1(c, grams, n):
                if n == 0:
                    pe.wait_ge(gram_out, grams)
                    pe.wait_ge(tail_out, 4 * c + 1)
                    pe.wait_ge(z1_kept, c + 1)
                    pe.wait_ge(z2_kept, c + 1)
                to = m_ps[:, n * P:(n + 1) * P]
                w = slice(n * P, (n + 1) * P)
                for k, z in enumerate((z1m, z2m, z3m)):
                    nc.tensor.matmul(to, wt1[:, k, w], z[:], start=(n == 0 and k == 0), stop=False,
                                     skip_group_check=True)
                d = bass.ds(c * P, P)
                last = nc.tensor.matmul(to, wt1d[:, w], dnt[:, d], start=False, stop=(n == N1 - 1),
                                        skip_group_check=True)
                if n == N1 - 1:
                    last.then_inc(tail_ready, 1)

            def tower2(c, grams, n):
                if n == 0:
                    pe.wait_ge(gram_out, grams)
                    pe.wait_ge(tail_out, 4 * c + 2)
                for k in range(N1):
                    last = nc.tensor.matmul(m_ps[:, n * P:(n + 1) * P], wt2[:, k, n * P:(n + 1) * P],
                                            h1s[:, k, :], start=(n == 0 and k == 0),
                                            stop=(n == N2 - 1 and k == N1 - 1), skip_group_check=True)
                if n == N2 - 1:
                    last.then_inc(tail_ready, 1)

            def tower3(c, grams):
                pe.wait_ge(gram_out, grams)
                pe.wait_ge(tail_out, 4 * c + 3)
                for k in range(N2):
                    last = nc.tensor.matmul(m_ps[0:1, 0:P], wt3[:, k:k + 1], h2s[:, k, :],
                                            start=(k == 0), stop=(k == N2 - 1))
                last.then_inc(tail_ready, 1)

            turn_dense()
            for piece in range(4):
                turn1_waits(0, piece, 0)
                if piece == 1:
                    pe.wait_ge(turned_out, 1)
                turn1(piece, (1 + piece) % 2)
            turn2_waits(0, 0, 0)
            turn2(0, 1)
            pe.wait_ge(ws_low, ZB)
            for k in range(ZB):
                z_turn(0, k, (6 + k) % 2,
                       (lambda: None) if k == 0 else (lambda: pe.wait_ge(turned_out, turn2_count(0, 0)))
                       if k == 1 else (lambda: bank_free(0, k - 2)))
                if k:
                    layer1(0, k - 1)
            layer1(0, ZB - 1)
            pe.wait_ge(w1_low, 1)
            pe.wait_ge(top_in, 96)
            pe.wait_ge(w2_in, 16)

            def chunk(c, first=False, last=False):
                bank = 13
                for q in range(GROUPS):
                    prep = not (last and q == GROUPS - 1)
                    g1 = c * GROUPS + q + 1
                    for s in range(SLOTS):
                        t, j = divmod(s, NBANK)
                        tile = c * TPC + q * TILES + t

                        def others():
                            if prep and q < 3 and s == 0:
                                turn2_waits(c, q + 1, g1)
                            if prep and q == 3 and s < 4:
                                turn1_waits(c + 1, s, g1)
                            if prep and q == 3 and s == 6:
                                turn2_waits(c + 1, 0, g1)

                        layer2(tile, q, t, j, g1, others)
                        if prep:
                            if q < 3 and s == 0:
                                turn2(q + 1, bank % 2)
                                bank += 1
                            if q == 3 and s < 4:
                                turn1(s, bank % 2)
                                bank += 1
                            if q == 3 and s == 6:
                                turn2(0, bank % 2)
                                bank += 1
                            k, r = divmod(s - TRANS0, STEP)
                            if r == 0 and 0 <= k < ZB:
                                def after():
                                    if k >= 2:
                                        bank_free(g1, k - 2)
                                    elif q == 3:
                                        pe.wait_ge(turned_out, turn2_count(c + 1, 0))
                                    else:
                                        pe.wait_ge(turned_out, turn2_count(c, q + 1))
                                        bank_free(g1, -1)
                                z_turn(g1, k, bank % 2, after)
                                bank += 1
                            k, r = divmod(s - TRANS0 - L1_LAG, STEP)
                            if r == 0 and 0 <= k < ZB:
                                layer1(g1, k)
                        if j == GRAM and not (first and q == 0 and t == 0):
                            between = not first and 1 <= q * TILES + t <= 4
                            gram(tile - 1, (t + 1) % 2, 4 * (c - 1) + q * TILES + t if between else None)
                        if not first:
                            if q == 0 and 9 <= s <= 16:
                                layer3(c - 1, 5 * (s - 9), 5 * (s - 8))
                            if q == 0 and 21 <= s < 21 + N1:
                                tower1(c - 1, TPC * c + 1, s - 21)
                            if q == 0 and 31 <= s < 31 + N2:
                                tower2(c - 1, TPC * c + 2, s - 31)
                            if q == 1 and s == 1:
                                tower3(c - 1, TPC * c + 3)

            chunk(0, first=True)
            with pe.Fori(1, NCHUNK - 1) as c:
                chunk(c)
            c = NCHUNK - 1
            chunk(c, last=True)
            n = NCHUNK * TPC
            gram(n - 1, 1, None)
            layer3(c, 0, NF)
            for i in range(N1):
                tower1(c, n, i)
            for i in range(N2):
                tower2(c, n, i)
            tower3(c, n)


def kernel(**inputs):
    import numpy as _np
    import concourse.bacc as _bacc
    from concourse import mybir as _mybir
    from concourse.bass_utils import run_bass_kernel_spmd as _run

    nc = _bacc.Bacc("TRN2", target_bir_lowering=False, num_devices=1)
    arrays = {}

    def given(name, a):
        a = _np.ascontiguousarray(a)
        arrays[f"in_{name}_dram"] = a
        return nc.dram_tensor(f"in_{name}_dram", a.shape, _mybir.dt.from_np(a.dtype), kind="ExternalInput").ap()

    identity = _np.eye(P, dtype=_np.float32)
    sample_mask = _np.repeat(_np.eye(BT, dtype=_np.float32), D, axis=0)

    args = [given(n, inputs[n]) for n in ("dense_ctx", "ids")]
    args.append([given(f"tbl_{f}", inputs[f"tbl_{f}"]) for f in range(NF)])
    args += [given("W_top1", inputs["W_top1"]),
             given("b_top1", _np.asarray(inputs["b_top1"]).reshape(N1, P).T),
             given("W_top2", inputs["W_top2"]),
             given("b_top2", _np.asarray(inputs["b_top2"]).reshape(N2, P).T),
             given("W_top3", _np.asarray(inputs["W_top3"]).reshape(N2, P).T)]
    args += [given(n, inputs[n]) for n in ("L0_rec_f0", "L0_rec_f1", "L0_rec_f2")]
    args += [given("identity", identity), given("sample_mask", sample_mask)]
    out = nc.dram_tensor("out_0_dram", (NB, 1), _mybir.dt.float32, kind="ExternalOutput").ap()
    build(nc, *args, out)
    r = _run(nc, [arrays], core_ids=[0])
    return r.results[0]["out_0_dram"]
```

```python
from contextlib import ExitStack

import concourse.bass as bass
from concourse import mybir

F32 = mybir.dt.float32
F32R = mybir.dt.float32r
I32 = mybir.dt.int32
ALU = mybir.AluOpType
ACT = mybir.ActivationFunctionType
AX_X = mybir.AxisListType.X

P = 128
NF = 39
D = 16
M = 128
NB = 512
NCHUNK = NB // P
GROUPS = 4
TILES = 4
BT = P // D
BG = BT * TILES
COLS = BG * D
TPC = GROUPS * TILES
HALF = TILES // 2

NK = NF // 2 + 1
KB = 3
NPROD = -(-NK // KB)
START = 3
PAIRS = NK * NF
ZB = -(-PAIRS // P)
REST = PAIRS - P * (ZB - 1)
R_HH, R_LH, R_HL = 0, 32, 64
XW = NF + NK - 1

FB = 4
KIND = "ADADADADAD"
NBANK = len(KIND)
SLOTS = TILES * NBANK
WIDTH = [min(FB, NF - FB * j) for j in range(NBANK)]
YB = 4
STT = sum(w for w, k in zip(WIDTH, KIND) if k == "D")
MUL = sum(w for w, k in zip(WIDTH, KIND) if k == "A")
NA = KIND.count("A")
ADDS = NA

STEP = 3
TURN2_SLOT = 1
LAST_TURN2_SLOT = 5
PRODUCT_SLOT = 5
TRANSPOSE_SLOT = PRODUCT_SLOT + STEP + 4
LOW_LAG = 1
L1_LAG = 5
C_SLOT = TRANSPOSE_SLOT + STEP * (ZB - 1) + L1_LAG
Z1_SLOT = 1

FINISH = 4
FINISH_LOW = 5
GRAM = 9

L3_SLOT, L3_STEP = 12, 7
KEEP_Z2_SLOT = 10
Z3_SLOT = 17
TOWER1_SLOT, H1_SLOT = 22, 26
TOWER2_SLOT, H2_SLOT = 33, 35
TOWER3_SLOT, Y_SLOT = 3, 4
KEEP_Z1_SLOT = 10

GATHERS = (4, 7, 6, 3, 3, 3, 3, 3, 3, 2, 2)
FIRST_GATHERS = (4, 4, 4, 3, 4, 3, 4, 3, 4, 3, 3)

H1, H2 = 512, 256
N1, N2 = H1 // P, H2 // P
ND = 16


def stt_count(tile, j):
    return tile * STT + sum(w for w, k in zip(WIDTH[:j + 1], KIND) if k == "D")


def mul_count(tile, j):
    return tile * MUL + sum(w for w, k in zip(WIDTH[:j + 1], KIND) if k == "A")


def krows(k):
    return min(P, PAIRS - P * k)


def build(nc, dense_ctx, ids, tables, w_top1, b_top1, w_top2, b_top2, w_top3, f0, f1, f2,
          identity, out):
    with ExitStack() as ctx:
        def sb(name, shape, dt=F32):
            return ctx.enter_context(nc.sbuf_tensor(name, shape, dt))

        def psum(name, shape):
            return ctx.enter_context(nc.psum_tensor(name, shape, F32))

        def sem(name):
            return ctx.enter_context(nc.semaphore(name))

        ident = sb("ident", [P, P])
        ids_sb = sb("ids_sb", [P, NF], I32)
        xg = sb("xg", [P, NF, D])
        xt = sb("xt", [NF, P * D])
        xs = sb("xs", [P, GROUPS, TILES, XW])
        xhl = sb("xhl", [P, GROUPS, TILES, 2, NF + 1], F32R)
        zp = sb("zp", [P, TILES, PAIRS])
        z_hi = sb("z_hi", [P, 3, COLS], F32R)
        z_lo = sb("z_lo", [P, 3, COLS], F32R)
        z_rest = sb("z_rest", [P, COLS], F32R)
        wr = sb("wr", [P, M], F32R)
        ws_hi = sb("ws_hi", [P, ZB - 1, M], F32R)
        ws_lo = sb("ws_lo", [P, ZB - 1, M], F32R)
        w1_hi = sb("w1_hi", [P, NF * M], F32R)
        w1_lo = sb("w1_lo", [P, NF * M], F32R)
        w2 = sb("w2", [P, NF, M])
        c_hi = sb("c_hi", [P, 2, COLS], F32R)
        c_lo = sb("c_lo", [P, 2, COLS], F32R)
        scaled = sb("scaled", [P, 2, NA, FB * M])
        flat = scaled[:].rearrange("p u a m -> p (u a m)")
        wab = flat[:, 0:2 * ZB * M].rearrange("p (o k m) -> p o k m", o=2, m=M)
        ws = flat[:, 2 * ZB * M:3 * ZB * M].rearrange("p (k m) -> p k m", m=M)
        psumg = sb("psumg", [P, 2, FB * M])
        part = sb("part", [P, 2, 4, M])
        half = sb("half", [P, 2, 2, M])
        cur2 = sb("cur2", [P, 2, M])
        cur2_hi = sb("cur2_hi", [P, 2, M], F32R)
        cur2_lo = sb("cur2_lo", [P, 2, M], F32R)
        xd = sb("xd", [P, 2, HALF, BT, 2, NF + 1], F32R)
        gs = sb("gs", [P, NF + 1, P])
        w1 = gs[:, 0:NF, :].rearrange("p f m -> p (f m)")
        z1 = sb("z1", [P, P])
        z1m = sb("z1m", [P, P])
        z2m = sb("z2m", [P, P])
        z3m = sb("z3m", [P, P])
        wt1 = sb("wt1", [P, 3, H1])
        wt1d = sb("wt1d", [ND, H1])
        wt2 = sb("wt2", [P, N1, H2])
        wt3 = sb("wt3", [P, N2])
        b1 = sb("b1", [P, N1])
        b2 = sb("b2", [P, N2])
        dn = sb("dn", [P, NCHUNK, ND])
        dnt = sb("dnt", [ND, NB])
        h1s = sb("h1s", [P, N1, P])
        h2s = sb("h2s", [P, N2, P])
        ysb = sb("ysb", [1, NB])

        y_ps = psum("y_ps", [P, YB, FB * M])
        t_ps = psum("t_ps", [P, 2, COLS])
        c_ps = psum("c_ps", [P, COLS])
        m_ps = psum("m_ps", [P, COLS])

        ident_in = sem("ident_in")
        pairs_in = sem("pairs_in")
        pairs_zero = sem("pairs_zero")
        w1_in = sem("w1_in")
        w2_in = sem("w2_in")
        top_in = sem("top_in")
        dense_in = sem("dense_in")
        ids_in = sem("ids_in")
        gathered = sem("gathered")
        zeros_set = sem("zeros_set")
        ws_sum = sem("ws_sum")
        ws_high = sem("ws_high")
        ws_low = sem("ws_low")
        w1_high = sem("w1_high")
        w1_low = sem("w1_low")
        turned = sem("turned")
        turned_out = sem("turned_out")
        early = sem("early")
        early_out = sem("early_out")
        early_products = sem("early_products")
        multiplied = sem("multiplied")
        z_turned = sem("z_turned")
        z_high = sem("z_high")
        z_low = sem("z_low")
        l1_step = sem("l1_step")
        c_high = sem("c_high")
        c_low = sem("c_low")
        z1_sum = sem("z1_sum")
        z1_kept = sem("z1_kept")
        y_ready = sem("y_ready")
        stt_done = sem("stt_done")
        mul_done = sem("mul_done")
        add_done = sem("add_done")
        half_done = sem("half_done")
        cur2_ready = sem("cur2_ready")
        cur2_high = sem("cur2_high")
        cur2_low = sem("cur2_low")
        x_low = sem("x_low")
        xd_zero = sem("xd_zero")
        xd_ready = [sem("xd_first"), sem("xd_second")]
        gram_ready = sem("gram_ready")
        gram_out = sem("gram_out")
        z2_kept = sem("z2_kept")
        tail_ready = sem("tail_ready")
        tail_out = sem("tail_out")
        y_out = sem("y_out")

        def wait(eng, s, n):
            if not isinstance(n, int) or n > 0:
                eng.wait_ge(s, n)

        def turn1_count(chunk, piece):
            early_group = 0 if isinstance(chunk, int) and chunk == 0 else 1
            return chunk * 8 + 1 + piece + 1 - early_group

        def turn2_count(chunk, q):
            return chunk * 8 + 5 + q

        def product_count(g, n):
            return (g - 1) * NPROD + START + n

        def product_views(q, k):
            nk = min(KB, NK - KB * k)
            w = xs[:, q, :, KB * k:KB * k + nk + NF - 1]
            ahead = bass.AP(tensor=w.tensor, offset=w.offset, ap=[w.ap[0], w.ap[1], [1, nk], [1, NF]])
            of = xs[:, q, :, 0:NF].unsqueeze(2).to_broadcast([P, TILES, nk, NF])
            to = zp[:, :, KB * NF * k:KB * NF * k + nk * NF].rearrange("p t (k f) -> p t k f", f=NF)
            return to, of, ahead

        out_rows = out.rearrange("b o -> o b")

        def pair_loads():
            for k in range(NK):
                for lo, hi in ((0, NF - k), (NF - k, NF)):
                    while lo < hi:
                        kb, row = divmod(k * NF + lo, P)
                        n = min(hi - lo, P - row)
                        g = (lo + k) % NF
                        first, second = sorted((lo * NF + g, g * NF + lo))
                        orders = 2 if k else 1
                        yield (wab[row:row + n, 0:orders, kb, :],
                               bass.AP(tensor=f0.tensor, offset=f0.offset + first * M,
                                       ap=[[(NF + 1) * M, n], [(second - first) * M if k else M, orders],
                                           [1, M]]))
                        lo += n

        pair_list = list(pair_loads())

        block = ctx.enter_context(nc.Block())

        @block.sync
        def _(sp):
            def spread(c, h):
                q, t = divmod(h * HALF, TILES)
                if isinstance(c, int) and c == 0 and h < 2:
                    sp.wait_ge(x_low, 1)
                wait(sp, gram_ready, c * TPC + HALF * (h - 1))
                for b in range(BT):
                    rows = slice(b * D, (b + 1) * D)
                    sp.dma_start(xd[rows, h % 2, :, b, :, :].bitcast(F32),
                                 xhl[rows, q, t:t + HALF, :, :].bitcast(F32)).then_inc(xd_ready[h % 2], 16)

            sp.dma_start(ids_sb[:], ids[0:P]).then_inc(ids_in, 16)
            sp.dma_start(ident[:], identity).then_inc(ident_in, 16)
            sp.dma_start(gs[:, 0:NF, :],
                         f1.rearrange("(f g) m -> g f m", g=P)).then_inc(w1_in, 16)
            sp.dma_start(dn[:], dense_ctx.rearrange("(c p) n -> p c n", p=P)).then_inc(dense_in, 16)
            sp.wait_ge(pairs_zero, 1)
            for to, of in pair_list:
                sp.dma_start(to, of).then_inc(pairs_in, 16)
            sp.dma_start(w2[:], f2.rearrange("(f g) m -> g f m", g=P)).then_inc(w2_in, 16)
            sp.dma_start(wt1[:], w_top1[0:3 * M, :].rearrange("(k p) n -> p k n", p=P)).then_inc(top_in, 16)
            sp.dma_start(wt1d[:], w_top1[3 * M:3 * M + ND, :]).then_inc(top_in, 16)
            sp.dma_start(wt2[:], w_top2.rearrange("(k p) n -> p k n", p=P)).then_inc(top_in, 16)
            sp.dma_start(wt3[:], w_top3).then_inc(top_in, 16)
            sp.dma_start(b1[:], b_top1).then_inc(top_in, 16)
            sp.dma_start(b2[:], b_top2).then_inc(top_in, 16)
            sp.wait_ge(xd_zero, 1)

            def chunk(c):
                for h in range(GROUPS * TILES // HALF):
                    spread(c, h)

            chunk(0)
            with sp.Fori(1, NCHUNK) as c:
                chunk(c)
            sp.wait_ge(y_out, 16 * NCHUNK)

        @block.gpsimd
        def _(pool):
            def gather(feats):
                for f in feats:
                    nc.gpsimd.indirect_dma_start(
                        xg[:, f, :], None, tables[f],
                        bass.IndirectOffsetOnAxis(ap=ids_sb[:, f:f + 1], axis=0)).then_inc(gathered, 16)

            nc.gpsimd.memset(wab[:, 1, :, :], 0.0).then_inc(pairs_zero, 1)
            nc.gpsimd.memset(xhl[:, :, :, 0, NF:].bitcast(F32), 1.0)
            nc.gpsimd.memset(xhl[:, :, :, 1, NF:].bitcast(F32), 0.0)
            nc.gpsimd.memset(z_rest[:].bitcast(F32), 0.0)
            nc.gpsimd.memset(wr[:].bitcast(F32), 0.0).then_inc(zeros_set, 1)
            pool.wait_ge(ids_in, 16)
            gather(range(NF))
            pool.wait_ge(early_out, 2)
            for k in range(START, NPROD):
                to, of, ahead = product_views(0, k)
                nc.gpsimd.tensor_tensor(to, of, ahead, ALU.mult).then_inc(early_products, 1)

            def chunk(c, first=False, last=False):
                for q in range(GROUPS):
                    for t in range(TILES):
                        tile = c * TPC + q * TILES + t
                        u = t % 2
                        n = q * TILES + t
                        counts = FIRST_GATHERS if first else GATHERS
                        feats = () if last else range(sum(counts[:n]), sum(counts[:n + 1]))
                        behind = [feats[len(feats) * i // ADDS:len(feats) * (i + 1) // ADDS]
                                  for i in range(ADDS)] if n else [()] * (ADDS - 1) + [feats]
                        for a in range(1, NA):
                            pool.wait_ge(mul_done, tile * MUL + FB * (a + 1))
                            wait(pool, add_done, tile * ADDS + a - 1)
                            prev = scaled[:, u, 0, :] if a == 1 else psumg[:, (a - 1) % 2, :]
                            nc.gpsimd.tensor_tensor(psumg[:, a % 2, :], prev, scaled[:, u, a, :],
                                                    ALU.add).then_inc(add_done, 1)
                            gather(behind[a - 1])
                        pool.wait_ge(add_done, tile * ADDS + ADDS - 1)
                        wait(pool, cur2_ready, tile - 1)
                        if q == 0 and t == 0 and not last:
                            pool.wait_ge(ids_in, 16 * (c + 2))
                            pool.wait_ge(turned, turn1_count(c, 3))
                        g = psumg[:, (NA - 1) % 2, :].rearrange("p (h m) -> p h m", m=2 * M)
                        nc.gpsimd.tensor_tensor(
                            part[:, u, 2:4, :].rearrange("p h m -> p (h m)"),
                            g[:, 0, :], g[:, 1, :], ALU.add).then_inc(add_done, 1)
                        gather(behind[-1])

            chunk(0, first=True)
            with pool.Fori(1, NCHUNK - 1) as c:
                chunk(c)
            chunk(NCHUNK - 1, last=True)

        @block.scalar
        def _(act):
            def turned_dense():
                act.wait_ge(turned, 1)
                nc.scalar.copy(dnt[:], t_ps[0:ND, 0, :]).then_inc(turned_out, 1)

            def turn1_out(chunk, piece, of):
                act.wait_ge(turned, turn1_count(chunk, piece))
                to = xt[:].rearrange("f (b d) -> f d b", d=D)[:, 4 * piece:4 * piece + 4, :]
                nc.scalar.copy(to, of.rearrange("f (d b) -> f d b", b=P)).then_inc(turned_out, 1)

            def group_out(q, bank):
                of = t_ps[:, bank, 0:TILES * NF].rearrange("p (t f) -> p t f", f=NF)
                nc.scalar.copy(xs[:, q, :, 0:NF], of)
                nc.scalar.copy(xs[:, q, :, NF:XW], of[:, :, 0:XW - NF])
                return nc.scalar.copy(xhl[:, q, :, 0, 0:NF], of)

            def turn2_out(chunk, q, bank):
                act.wait_ge(turned, turn2_count(chunk, q))
                group_out(q, bank).then_inc(turned_out, 1)

            def early_group_out():
                act.wait_ge(early, 1)
                nc.scalar.copy(xt[:, 0:COLS].rearrange("f (b d) -> f d b", d=D),
                               t_ps[0:NF, 1, :].rearrange("f (d b) -> f d b", b=BG)
                               ).then_inc(early_out, 1)
                act.wait_ge(early, 2)
                group_out(0, 0).then_inc(early_out, 1)

            def z_high_out(g, k, bank):
                act.wait_ge(z_turned, g * ZB + k + 1)
                wait(act, l1_step, g * ZB + k - 2 if 3 <= k < ZB - 1 else g * ZB)
                of = t_ps[0:krows(k), bank, :]
                if k < ZB - 1:
                    nc.scalar.copy(z_hi[:, k % 3, :], of).then_inc(z_high, 1)
                else:
                    nc.scalar.copy(z_rest[R_LH:R_LH + REST, :], of)
                    nc.scalar.copy(z_rest[R_HH:R_HH + REST, :], of).then_inc(z_high, 1)

            def c_high_out(g, u):
                act.wait_ge(l1_step, (g + 1) * ZB)
                nc.scalar.copy(c_hi[:, u, :], c_ps[:]).then_inc(c_high, 1)

            def cur2_high_out(tile, u):
                act.wait_ge(cur2_ready, tile + 1)
                wait(act, gram_ready, tile - 1)
                nc.scalar.copy(cur2_hi[:, u, :], cur2[:, u, :]).then_inc(cur2_high, 1)

            def keep_z1(c):
                act.wait_ge(z1_sum, GROUPS * (c + 1))
                nc.scalar.copy(z1m[:], z1[:]).then_inc(z1_kept, 1)

            def gram_read(tile, b0):
                act.wait_ge(gram_ready, tile + 1)
                nc.scalar.copy(gs[:, :, b0:b0 + BT],
                               m_ps[:, 0:BT * (NF + 1)].rearrange("p (b f) -> p f b", f=NF + 1)
                               ).then_inc(gram_out, 1)

            def keep_z2(c):
                act.wait_ge(gram_out, TPC * (c + 1))
                nc.scalar.copy(z2m[:], gs[:, NF, :]).then_inc(z2_kept, 1)

            def z3_out(c):
                act.wait_ge(tail_ready, 4 * c + 1)
                nc.scalar.copy(z3m[:], m_ps[:, 0:P]).then_inc(tail_out, 1)

            def h1_out(c, of=m_ps[:]):
                act.wait_ge(tail_ready, 4 * c + 2)
                for n in range(N1):
                    last = nc.scalar.activation(h1s[:, n, :], of[:, n * P:(n + 1) * P], ACT.Relu,
                                                bias=b1[:, n:n + 1])
                last.then_inc(tail_out, 1)

            def h2_out(c):
                act.wait_ge(tail_ready, 4 * c + 3)
                for n in range(N2):
                    last = nc.scalar.activation(h2s[:, n, :], m_ps[:, n * P:(n + 1) * P], ACT.Relu,
                                                bias=b2[:, n:n + 1])
                last.then_inc(tail_out, 1)

            def y_read(c):
                act.wait_ge(tail_ready, 4 * c + 4)
                nc.scalar.copy(ysb[:, bass.ds(c * P, P)], m_ps[0:1, 0:P]).then_inc(tail_out, 1)

            def send(c):
                act.wait_ge(tail_out, 4 * c + 4)
                act.dma_start(out_rows[:, bass.ds(c * P, P)], ysb[:, bass.ds(c * P, P)]).then_inc(y_out, 16)

            def load_ids(c):
                act.dma_start(ids_sb[:], ids[bass.ds(c * P, P)]).then_inc(ids_in, 16)

            def multiply(tile, q, t, j):
                a = KIND[:j].count("A")
                act.wait_ge(y_ready, tile * NBANK + j + 1)
                wait(act, add_done, (tile - 2) * ADDS + max(a, 1))
                for i in range(FB):
                    f = FB * j + i
                    nc.scalar.activation(
                        scaled[:, t % 2, a, i * M:(i + 1) * M],
                        y_ps[:, (t * NBANK + j) % YB, i * M:(i + 1) * M], ACT.Copy,
                        scale=xs[:, q, t, f:f + 1]).then_inc(mul_done, 1)

            turned_dense()
            act.wait_ge(w1_in, 16)
            nc.scalar.copy(w1_hi[:], w1).then_inc(w1_high, 1)
            act.wait_ge(ws_sum, 1)
            act.wait_ge(zeros_set, 1)
            nc.scalar.copy(ws_hi[:], ws[:, 0:ZB - 1, :])
            for row in (R_HH, R_HL):
                last = nc.scalar.copy(wr[row:row + REST, :], ws[0:REST, ZB - 1, :])
            last.then_inc(ws_high, 1)
            early_group_out()
            for k in range(ZB):
                z_high_out(0, k, k % 2)
            c_high_out(0, 0)
            for piece in range(4):
                turn1_out(0, piece, y_ps[0:NF, piece, :])
            act.wait_ge(top_in, 96)

            def chunk(c, first=False, last=False):
                bank = 1
                for q in range(GROUPS):
                    prep = not (last and q == GROUPS - 1)
                    g1 = c * GROUPS + q + 1
                    for s in range(SLOTS):
                        t, j = divmod(s, NBANK)
                        tile = c * TPC + q * TILES + t
                        if q == 0 and s == 0 and not last:
                            load_ids(c + 1)
                        if q == GROUPS - 1 and s == KEEP_Z1_SLOT:
                            keep_z1(c)
                        if KIND[j] == "A":
                            multiply(tile, q, t, j)
                        if j == 0 and not (first and q == 0 and t < 2):
                            gram_read(tile - 2, (q * BG + (t - 2) * BT) % P)
                        if prep:
                            if q < 3 and s == TURN2_SLOT:
                                turn2_out(c, q + 1, bank % 2)
                                bank += 1
                            if q == 3 and s < 4:
                                turn1_out(c + 1, s, t_ps[0:NF, bank % 2, :])
                                bank += 1
                            if q == 3 and s == LAST_TURN2_SLOT:
                                turn2_out(c + 1, 0, bank % 2)
                                bank += 1
                            k, r = divmod(s - TRANSPOSE_SLOT, STEP)
                            if r == 0 and 0 <= k < ZB:
                                z_high_out(g1, k, bank % 2)
                                bank += 1
                            if s == C_SLOT:
                                c_high_out(g1, (q + 1) % 2)
                        if j == FINISH and not (first and q == 0 and t == 0):
                            cur2_high_out(tile - 1, (t + 1) % 2)
                        if not first:
                            if q == 0 and s == KEEP_Z2_SLOT:
                                keep_z2(c - 1)
                            if q == 0 and s == Z3_SLOT:
                                z3_out(c - 1)
                            if q == 0 and s == H1_SLOT:
                                h1_out(c - 1)
                            if q == 0 and s == H2_SLOT:
                                h2_out(c - 1)
                            if q == 1 and s == Y_SLOT:
                                y_read(c - 1)
                                send(c - 1)

            chunk(0, first=True)
            with act.Fori(1, NCHUNK - 1) as c:
                chunk(c)
            c = NCHUNK - 1
            chunk(c, last=True)
            gram_read(NCHUNK * TPC - 2, P - 2 * BT)
            cur2_high_out(NCHUNK * TPC - 1, 1)
            gram_read(NCHUNK * TPC - 1, P - BT)
            keep_z2(c)
            z3_out(c)
            h1_out(c, t_ps[:, 0, :])
            h2_out(c)
            y_read(c)
            send(c)

        @block.vector
        def _(dve):
            def products(g, k, q):
                if k == 0:
                    if isinstance(g, int) and g == 0:
                        dve.wait_ge(early_out, 2)
                    else:
                        dve.wait_ge(turned_out, turn2_count(*q))
                    wait(dve, z_turned, g * ZB)
                to, of, ahead = product_views(q[1], k)
                nc.vector.tensor_tensor(to, of, ahead, ALU.mult).then_inc(multiplied, 1)
                if k == 0:
                    nc.vector.tensor_tensor(xhl[:, q[1], :, 1, 0:NF], xs[:, q[1], :, 0:NF],
                                            xhl[:, q[1], :, 0, 0:NF].bitcast(F32),
                                            ALU.subtract).then_inc(x_low, 1)

            def z_low_out(g, k, bank):
                dve.wait_ge(z_high, g * ZB + k + 1)
                r = krows(k)
                high, low = z_hi[:, k % 3, :], z_lo[:, k % 3, :]
                if k == ZB - 1:
                    high, low = z_rest[R_HH:R_HH + REST, :], z_rest[R_HL:R_HL + REST, :]
                nc.vector.tensor_tensor(low, t_ps[0:r, bank, :], high.bitcast(F32),
                                        ALU.subtract).then_inc(z_low, 1)

            def c_low_out(g, u):
                dve.wait_ge(c_high, g + 1)
                nc.vector.tensor_tensor(c_lo[:, u, :], c_ps[:], c_hi[:, u, :].bitcast(F32),
                                        ALU.subtract).then_inc(c_low, 1)

            def z1_out(g, q, kept):
                dve.wait_ge(l1_step, (g + 1) * ZB)
                wait(dve, z1_kept, kept)
                nc.vector.tensor_reduce(z1[:, q * BG:(q + 1) * BG],
                                        c_ps[:].rearrange("m (b d) -> m b d", d=D), AX_X,
                                        ALU.add).then_inc(z1_sum, 1)

            def accumulate(tile, q, t, j):
                dve.wait_ge(y_ready, tile * NBANK + j + 1)
                done = stt_count(0, j) - WIDTH[j]
                for i in range(WIDTH[j]):
                    n = done + i
                    f = FB * j + i
                    y = y_ps[:, (t * NBANK + j) % YB, i * M:(i + 1) * M]
                    to = part[:, t % 2, n % 2, :]
                    x = xs[:, q, t, f:f + 1]
                    if n < 2:
                        wait(dve, half_done, tile - 1)
                        nc.vector.tensor_scalar(to, y, x, None, ALU.mult).then_inc(stt_done, 1)
                    else:
                        dve.wait_ge(stt_done, tile * STT + n - 1)
                        nc.vector.scalar_tensor_tensor(out=to, in0=y, scalar=x, in1=to, op0=ALU.mult,
                                                       op1=ALU.add).then_inc(stt_done, 1)

            def finish(tile, u):
                dve.wait_ge(stt_done, (tile + 1) * STT)
                dve.wait_ge(add_done, (tile + 1) * ADDS)
                nc.vector.tensor_tensor(half[:, u, :, :], part[:, u, 0:2, :], part[:, u, 2:4, :],
                                        ALU.add).then_inc(half_done, 1)
                dve.wait_ge(half_done, tile + 1)
                wait(dve, gram_ready, tile - 1)
                nc.vector.tensor_tensor(cur2[:, u, :], half[:, u, 0, :], half[:, u, 1, :],
                                        ALU.add).then_inc(cur2_ready, 1)

            def cur2_low_out(tile, u):
                dve.wait_ge(cur2_high, tile + 1)
                nc.vector.tensor_tensor(cur2_lo[:, u, :], cur2[:, u, :], cur2_hi[:, u, :].bitcast(F32),
                                        ALU.subtract).then_inc(cur2_low, 1)

            nc.vector.memset(xd[:].bitcast(F32), 0.0).then_inc(xd_zero, 1)
            dve.wait_ge(w1_high, 1)
            nc.vector.tensor_tensor(w1_lo[:], w1, w1_hi[:].bitcast(F32), ALU.subtract).then_inc(w1_low, 1)
            dve.wait_ge(pairs_in, 16 * len(pair_list))
            nc.vector.tensor_tensor(ws[:, 0:ZB - 1, :], wab[:, 0, 0:ZB - 1, :], wab[:, 1, 0:ZB - 1, :],
                                    ALU.add)
            nc.vector.tensor_tensor(ws[0:REST, ZB - 1, :], wab[0:REST, 0, ZB - 1, :],
                                    wab[0:REST, 1, ZB - 1, :], ALU.add).then_inc(ws_sum, 1)
            dve.wait_ge(ws_high, 1)
            nc.vector.tensor_tensor(ws_lo[:], ws[:, 0:ZB - 1, :], ws_hi[:].bitcast(F32), ALU.subtract)
            nc.vector.tensor_tensor(wr[R_LH:R_LH + REST, :], ws[0:REST, ZB - 1, :],
                                    wr[R_HH:R_HH + REST, :].bitcast(F32), ALU.subtract).then_inc(ws_low, 1)
            for k in range(START):
                products(0, k, (0, 0))
            for k in range(ZB):
                z_low_out(0, k, k % 2)
            c_low_out(0, 0)

            def chunk(c, first=False, last=False):
                bank = 1
                for q in range(GROUPS):
                    prep = not (last and q == GROUPS - 1)
                    g1 = c * GROUPS + q + 1
                    nxt = (c, q + 1) if q < 3 else (c + 1, 0)
                    if prep:
                        bank += 5 if q == 3 else 1
                    for s in range(SLOTS):
                        t, j = divmod(s, NBANK)
                        tile = c * TPC + q * TILES + t
                        if KIND[j] == "D":
                            accumulate(tile, q, t, j)
                        if prep:
                            k, r = divmod(s - PRODUCT_SLOT, STEP)
                            if r == 0 and 0 <= k < NPROD:
                                products(g1, k, nxt)
                            k, r = divmod(s - TRANSPOSE_SLOT - LOW_LAG, STEP)
                            if r == 0 and 0 <= k < ZB:
                                z_low_out(g1, k, bank % 2)
                                bank += 1
                            if s == C_SLOT + 1:
                                c_low_out(g1, (q + 1) % 2)
                        if s == Z1_SLOT:
                            z1_out(c * GROUPS + q, q, c)
                        if j == FINISH and not (first and q == 0 and t == 0):
                            finish(tile - 1, (t + 1) % 2)
                        if j == FINISH_LOW and not (first and q == 0 and t == 0):
                            cur2_low_out(tile - 1, (t + 1) % 2)

            chunk(0, first=True)
            with dve.Fori(1, NCHUNK - 1) as c:
                chunk(c)
            chunk(NCHUNK - 1, last=True)
            finish(NCHUNK * TPC - 1, 1)
            cur2_low_out(NCHUNK * TPC - 1, 1)

        @block.tensor
        def _(pe):
            def bank_free(g, k):
                if k < 0:
                    g, k = g - 1, k + ZB
                wait(pe, z_low, g * ZB + k + 1)

            def turn_dense():
                pe.wait_ge(dense_in, 16)
                pe.wait_ge(ident_in, 16)
                for c in range(NCHUNK):
                    last = nc.tensor.transpose(t_ps[0:ND, 0, c * P:(c + 1) * P], dn[:, c, :], ident[:])
                last.then_inc(turned, 1)

            def turn1_waits(chunk, piece, g):
                if piece == 0:
                    pe.wait_ge(gathered, 16 * NF * (chunk + 1))
                if piece < 2:
                    bank_free(g, piece - 2)
                else:
                    pe.wait_ge(turned_out, turn1_count(chunk, piece - 2))

            def turn2_waits(chunk, q, g):
                pe.wait_ge(turned_out, turn1_count(chunk, 3))
                bank_free(g, -2)

            def turn1(piece, to):
                for i in range(4):
                    d = 4 * piece + i
                    last = nc.tensor.transpose(to[:, i * P:(i + 1) * P], xg[:, :, d], ident[:])
                last.then_inc(turned, 1)

            def turn_early():
                pe.wait_ge(gathered, 16 * NF)
                for d in range(D):
                    last = nc.tensor.transpose(t_ps[0:NF, 1, d * BG:(d + 1) * BG], xg[0:BG, :, d],
                                               ident[0:BG, 0:BG])
                last.then_inc(early, 1)
                pe.wait_ge(turned_out, 1)
                pe.wait_ge(early_out, 1)
                turn2(0, 0, early)

            def turn2(q, bank, done=turned):
                for t in range(TILES):
                    a = (q * TILES + t) * P
                    last = nc.tensor.transpose(t_ps[:, bank, t * NF:(t + 1) * NF], xt[:, a:a + P],
                                               ident[0:NF, 0:NF])
                last.then_inc(done, 1)

            def z_turn(g, k, bank, after):
                n = min(k + 2, NPROD)
                if isinstance(g, int) and g == 0:
                    pe.wait_ge(multiplied, min(n, START))
                    wait(pe, early_products, n - START)
                else:
                    pe.wait_ge(multiplied, product_count(g, n))
                after()
                r = krows(k)
                for t in range(TILES):
                    last = nc.tensor.transpose(t_ps[0:r, bank, t * P:(t + 1) * P], zp[:, t, P * k:P * k + r],
                                               ident[:])
                last.then_inc(z_turned, 1)

            def layer1(g, k):
                if k == 0:
                    wait(pe, z1_sum, g)
                    wait(pe, c_low, g)
                pe.wait_ge(z_high, g * ZB + k + 1)
                if k == ZB - 1:
                    pe.wait_ge(z_low, g * ZB + k + 1)
                    n = R_HL + REST
                    nc.tensor.matmul(c_ps[:], wr[0:n, :], z_rest[0:n, :], start=False,
                                     stop=True).then_inc(l1_step, 1)
                    return
                nc.tensor.matmul(c_ps[:], ws_hi[:, k, :], z_hi[:, k % 3, :], start=(k == 0), stop=False)
                nc.tensor.matmul(c_ps[:], ws_lo[:, k, :], z_hi[:, k % 3, :], start=False, stop=False)
                pe.wait_ge(z_low, g * ZB + k + 1)
                nc.tensor.matmul(c_ps[:], ws_hi[:, k, :], z_lo[:, k % 3, :], start=False,
                                 stop=False).then_inc(l1_step, 1)

            def layer2(tile, q, t, j, g, others=lambda: None):
                u = q % 2
                if t == 0 and j == 0:
                    pe.wait_ge(c_high, g)
                    pe.wait_ge(c_low, g)
                pj, pt = j - YB, tile
                if pj < 0:
                    pj, pt = pj + NBANK, tile - 1
                if isinstance(tile, int) and tile == 0 and j < YB:
                    pe.wait_ge(turned_out, turn1_count(0, j))
                elif KIND[pj] == "D":
                    wait(pe, stt_done, stt_count(pt, pj))
                else:
                    wait(pe, mul_done, mul_count(pt, pj))
                n = WIDTH[j] * M
                w = slice(FB * j * M, FB * j * M + n)
                to = y_ps[:, (t * NBANK + j) % YB, 0:n]
                hi = c_hi[:, u, t * P:(t + 1) * P]
                lo = c_lo[:, u, t * P:(t + 1) * P]
                nc.tensor.matmul(to, hi, w1_hi[:, w], start=True, stop=False)
                nc.tensor.matmul(to, hi, w1_lo[:, w], start=False, stop=False)
                others()
                nc.tensor.matmul(to, lo, w1_hi[:, w], start=False, stop=True).then_inc(y_ready, 1)

            def gram(tile, groups, n, tails):
                wait(pe, gram_out, tile)
                if tails is not None:
                    pe.wait_ge(tail_out, tails)
                pe.wait_ge(xd_ready[n // HALF % 2], 16 * BT * groups)
                pe.wait_ge(cur2_high, tile + 1)
                to = m_ps[:, 0:BT * (NF + 1)].rearrange("p (b f) -> p b f", f=NF + 1)
                u = n % 2
                x_hi, x_lo = (xd[:, n // HALF % 2, n % HALF, :, i, :] for i in range(2))
                nc.tensor.matmul(to, cur2_hi[:, u, :], x_hi, start=True, stop=False)
                nc.tensor.matmul(to, cur2_hi[:, u, :], x_lo, start=False, stop=False)
                pe.wait_ge(cur2_low, tile + 1)
                nc.tensor.matmul(to, cur2_lo[:, u, :], x_hi, start=False, stop=True
                                 ).then_inc(gram_ready, 1)

            def layer3(c, lo, hi):
                if lo == 0:
                    pe.wait_ge(gram_out, TPC * (c + 1))
                for f in range(lo, min(hi, NF)):
                    last = nc.tensor.matmul(m_ps[:, 0:P], w2[:, f, :], gs[:, f, :], start=(f == 0),
                                            stop=(f == NF - 1))
                if hi >= NF:
                    last.then_inc(tail_ready, 1)

            def tower1(c, grams, n):
                if n == 0:
                    pe.wait_ge(gram_out, grams)
                    pe.wait_ge(tail_out, 4 * c + 1)
                    pe.wait_ge(z1_kept, c + 1)
                    pe.wait_ge(z2_kept, c + 1)
                to = m_ps[:, n * P:(n + 1) * P]
                w = slice(n * P, (n + 1) * P)
                for k, z in enumerate((z1m, z2m, z3m)):
                    nc.tensor.matmul(to, wt1[:, k, w], z[:], start=(n == 0 and k == 0), stop=False,
                                     skip_group_check=True)
                d = bass.ds(c * P, P)
                last = nc.tensor.matmul(to, wt1d[:, w], dnt[:, d], start=False, stop=(n == N1 - 1),
                                        skip_group_check=True)
                if n == N1 - 1:
                    last.then_inc(tail_ready, 1)

            def last_tower1(c, parts, first=False, done=False):
                to = t_ps[:, 0, :].rearrange("m (n b) -> m n b", b=P)
                for n in range(N1):
                    w = slice(n * P, (n + 1) * P)
                    for weights, z in parts:
                        last = nc.tensor.matmul(to[:, n, :], weights[:, w], z,
                                                start=(first and n == 0 and z is parts[0][1]),
                                                stop=(done and n == N1 - 1), skip_group_check=True)
                if done:
                    last.then_inc(tail_ready, 1)

            def tower2(c, grams, n):
                if n == 0:
                    pe.wait_ge(gram_out, grams)
                    pe.wait_ge(tail_out, 4 * c + 2)
                for k in range(N1):
                    last = nc.tensor.matmul(m_ps[:, n * P:(n + 1) * P], wt2[:, k, n * P:(n + 1) * P],
                                            h1s[:, k, :], start=(n == 0 and k == 0),
                                            stop=(n == N2 - 1 and k == N1 - 1), skip_group_check=True)
                if n == N2 - 1:
                    last.then_inc(tail_ready, 1)

            def tower3(c, grams):
                pe.wait_ge(gram_out, grams)
                pe.wait_ge(tail_out, 4 * c + 3)
                for k in range(N2):
                    last = nc.tensor.matmul(m_ps[0:1, 0:P], wt3[:, k:k + 1], h2s[:, k, :],
                                            start=(k == 0), stop=(k == N2 - 1))
                last.then_inc(tail_ready, 1)

            turn_dense()
            turn_early()
            pe.wait_ge(ws_low, 1)
            for k in range(ZB):
                z_turn(0, k, k % 2, (lambda: pe.wait_ge(early_out, 2)) if k < 2 else
                       (lambda: bank_free(0, k - 2)))
                if k:
                    layer1(0, k - 1)
            turn1(0, y_ps[0:NF, 0, :])
            turn1(1, y_ps[0:NF, 1, :])
            layer1(0, ZB - 1)
            turn1(2, y_ps[0:NF, 2, :])
            turn1(3, y_ps[0:NF, 3, :])
            pe.wait_ge(w1_low, 1)
            pe.wait_ge(top_in, 96)
            pe.wait_ge(w2_in, 16)

            def chunk(c, first=False, last=False):
                bank = 1
                for q in range(GROUPS):
                    prep = not (last and q == GROUPS - 1)
                    g1 = c * GROUPS + q + 1
                    for s in range(SLOTS):
                        t, j = divmod(s, NBANK)
                        tile = c * TPC + q * TILES + t

                        def others():
                            if prep and q < 3 and s == TURN2_SLOT:
                                turn2_waits(c, q + 1, g1)
                            if prep and q == 3 and s < 4:
                                turn1_waits(c + 1, s, g1)
                            if prep and q == 3 and s == LAST_TURN2_SLOT:
                                turn2_waits(c + 1, 0, g1)

                        layer2(tile, q, t, j, g1, others)
                        if prep:
                            if q < 3 and s == TURN2_SLOT:
                                turn2(q + 1, bank % 2)
                                bank += 1
                            if q == 3 and s < 4:
                                turn1(s, t_ps[0:NF, bank % 2, :])
                                bank += 1
                            if q == 3 and s == LAST_TURN2_SLOT:
                                turn2(0, bank % 2)
                                bank += 1
                            k, r = divmod(s - TRANSPOSE_SLOT, STEP)
                            if r == 0 and 0 <= k < ZB:
                                def after():
                                    if k >= 2:
                                        bank_free(g1, k - 2)
                                    elif q == 3:
                                        pe.wait_ge(turned_out, turn2_count(c + 1, 0))
                                    else:
                                        pe.wait_ge(turned_out, turn2_count(c, q + 1))
                                        bank_free(g1, -1)
                                z_turn(g1, k, bank % 2, after)
                                bank += 1
                            k, r = divmod(s - TRANSPOSE_SLOT - L1_LAG, STEP)
                            if r == 0 and 0 <= k < ZB:
                                layer1(g1, k)
                        if j == GRAM and not (first and q == 0 and t == 0):
                            between = not first and 1 <= q * TILES + t <= 4
                            n = q * TILES + t - 1
                            gram(tile - 1, c * GROUPS + n // TILES + 1, n % TPC,
                                 4 * (c - 1) + n + 1 if between else None)
                        if not first:
                            if q == 0 and L3_SLOT <= s < L3_SLOT - (-NF // L3_STEP):
                                layer3(c - 1, L3_STEP * (s - L3_SLOT), L3_STEP * (s - L3_SLOT + 1))
                            if q == 0 and TOWER1_SLOT <= s < TOWER1_SLOT + N1:
                                tower1(c - 1, TPC * c + 1, s - TOWER1_SLOT)
                            if q == 0 and TOWER2_SLOT <= s < TOWER2_SLOT + N2:
                                tower2(c - 1, TPC * c + 2, s - TOWER2_SLOT)
                            if q == 1 and s == TOWER3_SLOT:
                                tower3(c - 1, TPC * c + 3)

            chunk(0, first=True)
            with pe.Fori(1, NCHUNK - 1) as c:
                chunk(c)
            c = NCHUNK - 1
            chunk(c, last=True)
            n = NCHUNK * TPC
            pe.wait_ge(z1_kept, NCHUNK)
            bank_free(NCHUNK * GROUPS - 1, ZB - 1)
            last_tower1(c, ((wt1[:, 0, :], z1m[:]), (wt1d[:], dnt[:, c * P:])), first=True)
            gram(n - 1, n // TILES, TPC - 1, None)
            layer3(c, 0, NF)
            pe.wait_ge(z2_kept, NCHUNK)
            last_tower1(c, ((wt1[:, 1, :], z2m[:]),))
            pe.wait_ge(tail_out, 4 * c + 1)
            last_tower1(c, ((wt1[:, 2, :], z3m[:]),), done=True)
            for i in range(N2):
                tower2(c, n, i)
            tower3(c, n)


def kernel(**inputs):
    import numpy as _np
    import concourse.bacc as _bacc
    from concourse import mybir as _mybir
    from concourse.bass_utils import run_bass_kernel_spmd as _run

    nc = _bacc.Bacc("TRN2", target_bir_lowering=False, num_devices=1)
    arrays = {}

    def given(name, a):
        a = _np.ascontiguousarray(a)
        arrays[f"in_{name}_dram"] = a
        return nc.dram_tensor(f"in_{name}_dram", a.shape, _mybir.dt.from_np(a.dtype), kind="ExternalInput").ap()

    identity = _np.eye(P, dtype=_np.float32)

    args = [given(n, inputs[n]) for n in ("dense_ctx", "ids")]
    args.append([given(f"tbl_{f}", inputs[f"tbl_{f}"]) for f in range(NF)])
    args += [given("W_top1", inputs["W_top1"]),
             given("b_top1", _np.asarray(inputs["b_top1"]).reshape(N1, P).T),
             given("W_top2", inputs["W_top2"]),
             given("b_top2", _np.asarray(inputs["b_top2"]).reshape(N2, P).T),
             given("W_top3", _np.asarray(inputs["W_top3"]).reshape(N2, P).T)]
    args += [given(n, inputs[n]) for n in ("L0_rec_f0", "L0_rec_f1", "L0_rec_f2")]
    args += [given("identity", identity)]
    out = nc.dram_tensor("out_0_dram", (NB, 1), _mybir.dt.float32, kind="ExternalOutput").ap()
    build(nc, *args, out)
    r = _run(nc, [arrays], core_ids=[0])
    return r.results[0]["out_0_dram"]
```

```python
from contextlib import ExitStack

import concourse.bass as bass
from concourse import mybir

F32 = mybir.dt.float32
F32R = mybir.dt.float32r
I32 = mybir.dt.int32
ALU = mybir.AluOpType
ACT = mybir.ActivationFunctionType
AX_X = mybir.AxisListType.X

P = 128
NF = 39
D = 16
M = 128
NB = 512
NCHUNK = NB // P
GROUPS = 4
TILES = 4
BT = P // D
BG = BT * TILES
COLS = BG * D
TPC = GROUPS * TILES
HALF = TILES // 2

NK = NF // 2 + 1
KB = 3
ZB = -(-NK // KB)
ROWS = KB * NF
RING = 4
POOL_BLOCKS = (3,)
BLOCKS = GROUPS * ZB
XW = NF + NK - 1

FB = 4
KIND = "ADADADADAD"
NBANK = len(KIND)
SLOTS = TILES * NBANK
WIDTH = [min(FB, NF - FB * j) for j in range(NBANK)]
YB = 4
STT = sum(w for w, k in zip(WIDTH, KIND) if k == "D")
MUL = sum(w for w, k in zip(WIDTH, KIND) if k == "A")
NA = KIND.count("A")
ADDS = NA

STEP = 3
TURN2_SLOT = 3
LAST_TURN2_SLOT = 5
TURN1_SLOTS = tuple(3 * SLOTS - 8 + 2 * i for i in range(4))
FIRST_TURN1_SLOTS = tuple(3 * SLOTS + i for i in range(4))


def turn1_piece(first, q, s):
    slots = FIRST_TURN1_SLOTS if first else TURN1_SLOTS
    return slots.index(q * SLOTS + s) if q * SLOTS + s in slots else None


def turn2_slot(first, q):
    return LAST_TURN2_SLOT if first and q == GROUPS - 1 else TURN2_SLOT


PRODUCT_SLOT = 9
HIGH_LAG = 1
LOW_LAG = 2
L1_LAG = 6
C_SLOT = PRODUCT_SLOT + STEP * (ZB - 1) + L1_LAG
Z1_SLOT = 1

FINISH = 4
FINISH_LOW = 5
GRAM = 9

L3_SLOT = 12
L3_STEP = 7
KEEP_Z2_SLOT = 10
Z3_SLOT = 17
TOWER1_SLOT = 22
H1_SLOT = 25
TOWER2_SLOT = 33
H2_SLOT = 35
TOWER3_SLOT = 3
Y_SLOT = 7
KEEP_Z1_SLOT = 10

AHEAD_TILE = 13
AHEAD = (3, 3, 3)
GATHERS = (2, 6, 4, 3, 3, 3, 3, 2, 2, 2)
FIRST_GATHERS = (4, 4, 4, 3, 4, 3, 4, 3, 4, 3, 3)
assert sum(AHEAD) + sum(GATHERS) == sum(FIRST_GATHERS) == NF

H1, H2 = 512, 256
N1, N2 = H1 // P, H2 // P
ND = 16


def stt_count(tile, j):
    return tile * STT + sum(w for w, k in zip(WIDTH[:j + 1], KIND) if k == "D")


def mul_count(tile, j):
    return tile * MUL + sum(w for w, k in zip(WIDTH[:j + 1], KIND) if k == "A")


def krows(k):
    return min(KB, NK - KB * k) * NF


def build(nc, dense_ctx, ids, tables, w_top1, b_top1, w_top2, b_top2, w_top3, f0, f1, f2,
          identity, out):
    with ExitStack() as ctx:
        def sb(name, shape, dt=F32):
            return ctx.enter_context(nc.sbuf_tensor(name, shape, dt))

        def psum(name, shape):
            return ctx.enter_context(nc.psum_tensor(name, shape, F32))

        def sem(name):
            return ctx.enter_context(nc.semaphore(name))

        ident = sb("ident", [P, P])
        ids_sb = sb("ids_sb", [P, NCHUNK * NF], I32)
        xg = sb("xg", [P, NF, D])
        xt = sb("xt", [XW, P * D])
        xs = sb("xs", [P, GROUPS, TILES, NF])
        xhl = sb("xhl", [P, GROUPS, TILES, 2, NF + 1], F32R)
        one_side = sb("one_side", [ROWS, 2, COLS])
        other_side = sb("other_side", [ROWS, RING, COLS])
        zp = sb("zp", [ROWS, 2, COLS])
        z_hi = sb("z_hi", [ROWS, 3, COLS], F32R)
        z_lo = sb("z_lo", [ROWS, 3, COLS], F32R)
        ws_hi = sb("ws_hi", [P, ZB, M], F32R)
        ws_lo = sb("ws_lo", [P, ZB, M], F32R)
        w1_hi = sb("w1_hi", [P, NF * M], F32R)
        w1_lo = sb("w1_lo", [P, NF * M], F32R)
        w2 = sb("w2", [P, NF, M])
        c_hi = sb("c_hi", [P, 2, COLS], F32R)
        c_lo = sb("c_lo", [P, 2, COLS], F32R)
        scaled = sb("scaled", [P, 2, NA, FB * M])
        flat = scaled[:].rearrange("p u a m -> p (u a m)")
        wab = flat[:, 0:2 * ZB * M].rearrange("p (o k m) -> p o k m", o=2, m=M)
        ws = flat[:, 2 * ZB * M:3 * ZB * M].rearrange("p (k m) -> p k m", m=M)
        psumg = sb("psumg", [P, 2, FB * M])
        part = sb("part", [P, 2, 4, M])
        half = sb("half", [P, 2, 2, M])
        cur2 = sb("cur2", [P, 2, M])
        cur2_hi = sb("cur2_hi", [P, 2, M], F32R)
        cur2_lo = sb("cur2_lo", [P, 2, M], F32R)
        xd = sb("xd", [P, 2, HALF, BT, 2, NF + 1], F32R)
        gs = sb("gs", [P, NF + 1, P])
        w1 = gs[:, 0:NF, :].rearrange("p f m -> p (f m)")
        z1 = sb("z1", [P, P])
        z1m = sb("z1m", [P, P])
        z2m = sb("z2m", [P, P])
        z3m = sb("z3m", [P, P])
        wt1 = sb("wt1", [P, 3, H1])
        wt1d = sb("wt1d", [ND, H1])
        wt2 = sb("wt2", [P, N1, H2])
        wt3 = sb("wt3", [P, N2])
        b1 = sb("b1", [P, N1])
        b2 = sb("b2", [P, N2])
        dn = sb("dn", [P, NCHUNK, ND])
        dnt = sb("dnt", [ND, NB])
        h1s = sb("h1s", [P, N1, P])
        h2s = sb("h2s", [P, N2, P])
        ysb = sb("ysb", [1, NB])

        y_ps = psum("y_ps", [P, YB, FB * M])
        t_ps = psum("t_ps", [P, 2, COLS])
        c_ps = psum("c_ps", [P, COLS])
        m_ps = psum("m_ps", [P, COLS])

        ident_in = sem("ident_in")
        pairs_in = sem("pairs_in")
        pairs_zero = sem("pairs_zero")
        w1_in = sem("w1_in")
        w2_in = sem("w2_in")
        top_in = sem("top_in")
        dense_in = sem("dense_in")
        ids_in = sem("ids_in")
        gathered = sem("gathered")
        ones_set = sem("ones_set")
        ws_sum = sem("ws_sum")
        ws_high = sem("ws_high")
        ws_low = sem("ws_low")
        w1_high = sem("w1_high")
        w1_low = sem("w1_low")
        turned = sem("turned")
        turned_out = sem("turned_out")
        early = sem("early")
        early_out = sem("early_out")
        again_in = sem("again_in")
        one_in = [sem(f"one_in{i}") for i in range(2)]
        other_in = [sem(f"other_in{i}") for i in range(RING)]
        early_one = sem("early_one")
        early_other = {k: sem(f"early_other{k}") for k in POOL_BLOCKS}
        multiplied = sem("multiplied")
        z_high = sem("z_high")
        z_low = sem("z_low")
        l1_step = sem("l1_step")
        c_high = sem("c_high")
        c_low = sem("c_low")
        z1_sum = sem("z1_sum")
        z1_kept = sem("z1_kept")
        y_ready = sem("y_ready")
        stt_done = sem("stt_done")
        mul_done = sem("mul_done")
        add_done = sem("add_done")
        half_done = sem("half_done")
        cur2_ready = sem("cur2_ready")
        cur2_high = sem("cur2_high")
        cur2_low = sem("cur2_low")
        x_low = sem("x_low")
        xd_zero = sem("xd_zero")
        xd_ready = [sem("xd_first"), sem("xd_second")]
        gram_ready = sem("gram_ready")
        gram_out = sem("gram_out")
        z2_kept = sem("z2_kept")
        tail_ready = sem("tail_ready")
        tail_out = sem("tail_out")
        y_out = sem("y_out")

        def wait(eng, s, n):
            if not isinstance(n, int) or n > 0:
                eng.wait_ge(s, n)

        def turn1_count(chunk, piece):
            early_group = 0 if isinstance(chunk, int) and chunk == 0 else 1
            return chunk * 8 + 1 + piece + 1 - early_group

        def turn2_count(chunk, q):
            return chunk * 8 + 5 + q

        def turn1_bank(piece):
            return (1 + piece) % 2

        def turn2_bank(q):
            return (5 + q) % 2

        def loads(k):
            return min(KB, NK - KB * k)

        def other_count(chunk, i):
            one_chunk = sum(loads(n % ZB) for n in range(i % RING, BLOCKS, RING))
            return 16 * (chunk * one_chunk + sum(loads(n % ZB) for n in range(i % RING, i + 1, RING))
                         - sum(loads(n) for n in POOL_BLOCKS if n % RING == i % RING and
                               (i >= n or not isinstance(chunk, int) or chunk > 0)))

        out_rows = out.rearrange("b o -> o b")

        def pair_loads():
            for k in range(NK):
                for lo, hi in ((0, NF - k), (NF - k, NF)):
                    if lo < hi:
                        kb, row, n = k // KB, k % KB * NF + lo, hi - lo
                        g = (lo + k) % NF
                        first, second = sorted((lo * NF + g, g * NF + lo))
                        orders = 2 if k else 1
                        yield (wab[row:row + n, 0:orders, kb, :],
                               bass.AP(tensor=f0.tensor, offset=f0.offset + first * M,
                                       ap=[[(NF + 1) * M, n], [(second - first) * M if k else M, orders],
                                           [1, M]]))

        pair_list = list(pair_loads())

        def lay_out_one(eng, q, done):
            for n in range(KB):
                eng.dma_start(one_side[n * NF:(n + 1) * NF, q % 2, :],
                              xt[0:NF, q * COLS:(q + 1) * COLS]).then_inc(done, 16)

        def lay_out_other(eng, c, q, k, done, agains=None):
            i = q * ZB + k
            wait(eng, multiplied, c * BLOCKS + i + 1 - RING)
            for n in range(loads(k)):
                first = KB * k + n
                if agains is not None and (first == 1 or (k > 0 and n == 0)):
                    eng.wait_ge(again_in, 16 * agains)
                eng.dma_start(other_side[n * NF:(n + 1) * NF, i % RING, :],
                              xt[first:first + NF, q * COLS:(q + 1) * COLS]
                              ).then_inc(done, 16)

        block = ctx.enter_context(nc.Block())

        @block.sync
        def _(sp):
            def spread(c, h):
                q, t = divmod(h * HALF, TILES)
                if isinstance(c, int) and c == 0 and h < 2:
                    sp.wait_ge(x_low, 1)
                wait(sp, gram_ready, c * TPC + HALF * (h - 1))
                for b in range(BT):
                    rows = slice(b * D, (b + 1) * D)
                    sp.dma_start(xd[rows, h % 2, :, b, :, :].bitcast(F32),
                                 xhl[rows, q, t:t + HALF, :, :].bitcast(F32)).then_inc(xd_ready[h % 2], 16)

            sp.dma_start(ids_sb[:].rearrange("p (c f) -> p c f", f=NF),
                         ids.rearrange("(c p) f -> p c f", p=P)).then_inc(ids_in, 16)
            sp.dma_start(ident[:], identity).then_inc(ident_in, 16)
            sp.dma_start(gs[:, 0:NF, :],
                         f1.rearrange("(f g) m -> g f m", g=P)).then_inc(w1_in, 16)
            sp.dma_start(dn[:], dense_ctx.rearrange("(c p) n -> p c n", p=P)).then_inc(dense_in, 16)
            sp.wait_ge(pairs_zero, 1)
            for to, of in pair_list:
                sp.dma_start(to, of).then_inc(pairs_in, 16)
            sp.dma_start(w2[:], f2.rearrange("(f g) m -> g f m", g=P)).then_inc(w2_in, 16)
            sp.dma_start(wt1[:], w_top1[0:3 * M, :].rearrange("(k p) n -> p k n", p=P)).then_inc(top_in, 16)
            sp.dma_start(wt1d[:], w_top1[3 * M:3 * M + ND, :]).then_inc(top_in, 16)
            sp.dma_start(wt2[:], w_top2.rearrange("(k p) n -> p k n", p=P)).then_inc(top_in, 16)
            sp.dma_start(wt3[:], w_top3).then_inc(top_in, 16)
            sp.dma_start(b1[:], b_top1).then_inc(top_in, 16)
            sp.dma_start(b2[:], b_top2).then_inc(top_in, 16)

            def lay_out(c, q, k, agains=None):
                if k == 0:
                    lay_out_one(sp, q, one_in[q % 2])
                lay_out_other(sp, c, q, k, other_in[(q * ZB + k) % RING], agains)

            def again(c, columns=slice(0, P * D)):
                if columns.stop == COLS:
                    sp.wait_ge(early_out, 1)
                else:
                    sp.wait_ge(turned_out, turn1_count(c, 3))
                sp.dma_start(xt[NF:XW, columns], xt[0:XW - NF, columns]).then_inc(again_in, 16)

            again(0, slice(0, COLS))
            for k in range(ZB):
                if k not in POOL_BLOCKS:
                    lay_out_other(sp, 0, 0, k, other_in[k % RING], 1 if k == 0 else None)
            again(0, slice(COLS, P * D))
            for k in range(RING):
                lay_out(0, 1, k, 2 if k == 0 else None)
            sp.wait_ge(xd_zero, 1)
            sp.wait_ge(ones_set, 1)

            def chunk(c, last=False):
                for q in range(GROUPS):
                    if q < 3:
                        spread(c, 2 * q)
                        spread(c, 2 * q + 1)
                    if q < 3 or not last:
                        to = (c, q + 1) if q < 3 else (c + 1, 0)
                        for k in range(RING, ZB):
                            lay_out(*to, k)
                    if q == 2:
                        spread(c, 2 * q + 2)
                    if q == 3:
                        spread(c, 2 * q + 1)
                    if q < 2 or not last:
                        to = (c, q + 2) if q < 2 else (c + 1, q - 2)
                        if q == 2:
                            again(c + 1)
                        for k in range(RING):
                            lay_out(*to, k, c + 3 if q == 2 and k == 0 else None)

            chunk(0)
            with sp.Fori(1, NCHUNK - 1) as c:
                chunk(c)
            chunk(NCHUNK - 1, last=True)
            sp.wait_ge(y_out, 16 * NCHUNK)

        @block.gpsimd
        def _(pool):
            def gather(chunk, feats):
                for f in feats:
                    nc.gpsimd.indirect_dma_start(
                        xg[:, f, :], None, tables[f],
                        bass.IndirectOffsetOnAxis(ap=ids_sb[:, bass.ds(chunk * NF + f, 1)], axis=0)
                    ).then_inc(gathered, 16)

            nc.gpsimd.memset(wab[:, 1, :, :], 0.0).then_inc(pairs_zero, 1)
            nc.gpsimd.memset(xhl[:, :, :, 0, NF:].bitcast(F32), 1.0)
            nc.gpsimd.memset(xhl[:, :, :, 1, NF:].bitcast(F32), 0.0).then_inc(ones_set, 1)
            pool.wait_ge(ids_in, 16)
            gather(0, range(NF))
            pool.wait_ge(early_out, 1)
            lay_out_one(pool, 0, early_one)
            for k in POOL_BLOCKS:
                lay_out_other(pool, 0, 0, k, early_other[k], 1 if k == POOL_BLOCKS[0] else None)

            def chunk_of(c, first=False, before_last=False, last=False):
                for q in range(GROUPS):
                    for t in range(TILES):
                        tile = c * TPC + q * TILES + t
                        u = t % 2
                        n = q * TILES + t
                        counts = FIRST_GATHERS if first else (sum(AHEAD),) + GATHERS
                        chunk, m = c + 1, n if first else n + 1
                        if n >= AHEAD_TILE:
                            counts, chunk, m = (0,) + AHEAD, c + 2, n - AHEAD_TILE + 1
                        feats = range(sum(counts[:m]), sum(counts[:m + 1]))
                        if last or (before_last and n >= AHEAD_TILE):
                            feats = ()
                        at_end = (first and n == 0) or n == AHEAD_TILE
                        behind = [feats[len(feats) * i // ADDS:len(feats) * (i + 1) // ADDS]
                                  for i in range(ADDS)] if not at_end else [()] * (ADDS - 1) + [feats]
                        for a in range(1, NA):
                            pool.wait_ge(mul_done, tile * MUL + FB * (a + 1))
                            wait(pool, add_done, tile * ADDS + a - 1)
                            prev = scaled[:, u, 0, :] if a == 1 else psumg[:, (a - 1) % 2, :]
                            nc.gpsimd.tensor_tensor(psumg[:, a % 2, :], prev, scaled[:, u, a, :],
                                                    ALU.add).then_inc(add_done, 1)
                            gather(chunk, behind[a - 1])
                        pool.wait_ge(add_done, tile * ADDS + ADDS - 1)
                        wait(pool, cur2_ready, tile - 1)
                        if at_end and feats:
                            pool.wait_ge(turned, turn1_count(chunk - 1, 3))
                        g = psumg[:, (NA - 1) % 2, :].rearrange("p (h m) -> p h m", m=2 * M)
                        nc.gpsimd.tensor_tensor(
                            part[:, u, 2:4, :].rearrange("p h m -> p (h m)"),
                            g[:, 0, :], g[:, 1, :], ALU.add).then_inc(add_done, 1)
                        gather(chunk, behind[-1])

            chunk_of(0, first=True)
            with pool.Fori(1, NCHUNK - 2) as c:
                chunk_of(c)
            chunk_of(NCHUNK - 2, before_last=True)
            chunk_of(NCHUNK - 1, last=True)

        @block.scalar
        def _(act):
            def turned_dense():
                act.wait_ge(turned, 1)
                nc.scalar.copy(dnt[:], t_ps[0:ND, 0, :]).then_inc(turned_out, 1)

            def turn1_out(chunk, piece, of):
                act.wait_ge(turned, turn1_count(chunk, piece))
                start = BG if isinstance(chunk, int) and chunk == 0 else 0
                to = xt[0:NF, :].rearrange("f (b d) -> f d b", d=D)[:, 4 * piece:4 * piece + 4, start:]
                nc.scalar.copy(to, of.rearrange("f (d b) -> f d b", b=P)[:, :, start:]
                               ).then_inc(turned_out, 1)

            def group_out(q, bank):
                of = t_ps[:, bank, 0:TILES * NF].rearrange("p (t f) -> p t f", f=NF)
                nc.scalar.copy(xs[:, q, :, 0:NF], of)
                return nc.scalar.copy(xhl[:, q, :, 0, 0:NF], of)

            def turn2_out(chunk, q, bank):
                act.wait_ge(turned, turn2_count(chunk, q))
                group_out(q, bank).then_inc(turned_out, 1)

            def early_group_out():
                act.wait_ge(early, 1)
                nc.scalar.copy(xt[0:NF, 0:COLS].rearrange("f (b d) -> f d b", d=D),
                               t_ps[0:NF, 1, :].rearrange("f (d b) -> f d b", b=BG)
                               ).then_inc(early_out, 1)
                act.wait_ge(early, 2)
                group_out(0, 0).then_inc(early_out, 1)

            def z_high_out(g, k, i):
                act.wait_ge(multiplied, g * ZB + k + 1)
                wait(act, l1_step, g * ZB + k - 2 if k >= 3 else g * ZB)
                r = krows(k)
                nc.scalar.copy(z_hi[0:r, k % 3, :], zp[0:r, i % 2, :]).then_inc(z_high, 1)

            def c_high_out(g, u):
                act.wait_ge(l1_step, (g + 1) * ZB)
                nc.scalar.copy(c_hi[:, u, :], c_ps[:]).then_inc(c_high, 1)

            def cur2_high_out(tile, u):
                act.wait_ge(cur2_ready, tile + 1)
                wait(act, gram_ready, tile - 1)
                nc.scalar.copy(cur2_hi[:, u, :], cur2[:, u, :]).then_inc(cur2_high, 1)

            def keep_z1(c):
                act.wait_ge(z1_sum, GROUPS * (c + 1))
                nc.scalar.copy(z1m[:], z1[:]).then_inc(z1_kept, 1)

            def gram_read(tile, b0):
                act.wait_ge(gram_ready, tile + 1)
                nc.scalar.copy(gs[:, :, b0:b0 + BT],
                               m_ps[:, 0:BT * (NF + 1)].rearrange("p (b f) -> p f b", f=NF + 1)
                               ).then_inc(gram_out, 1)

            def keep_z2(c):
                act.wait_ge(gram_out, TPC * (c + 1))
                nc.scalar.copy(z2m[:], gs[:, NF, :]).then_inc(z2_kept, 1)

            def z3_out(c):
                act.wait_ge(tail_ready, 4 * c + 1)
                nc.scalar.copy(z3m[:], m_ps[:, 0:P]).then_inc(tail_out, 1)

            def h1_out(c, of=m_ps[:]):
                act.wait_ge(tail_ready, 4 * c + 2)
                for n in range(N1):
                    last = nc.scalar.activation(h1s[:, n, :], of[:, n * P:(n + 1) * P], ACT.Relu,
                                                bias=b1[:, n:n + 1])
                last.then_inc(tail_out, 1)

            def h2_out(c):
                act.wait_ge(tail_ready, 4 * c + 3)
                for n in range(N2):
                    last = nc.scalar.activation(h2s[:, n, :], m_ps[:, n * P:(n + 1) * P], ACT.Relu,
                                                bias=b2[:, n:n + 1])
                last.then_inc(tail_out, 1)

            def y_read(c):
                act.wait_ge(tail_ready, 4 * c + 4)
                nc.scalar.copy(ysb[:, bass.ds(c * P, P)], m_ps[0:1, 0:P]).then_inc(tail_out, 1)

            def send(c):
                act.wait_ge(tail_out, 4 * c + 4)
                act.dma_start(out_rows[:, bass.ds(c * P, P)], ysb[:, bass.ds(c * P, P)]).then_inc(y_out, 16)

            def multiply(tile, q, t, j):
                a = KIND[:j].count("A")
                act.wait_ge(y_ready, tile * NBANK + j + 1)
                wait(act, add_done, (tile - 2) * ADDS + max(a, 1))
                for i in range(FB):
                    f = FB * j + i
                    nc.scalar.activation(
                        scaled[:, t % 2, a, i * M:(i + 1) * M],
                        y_ps[:, (t * NBANK + j) % YB, i * M:(i + 1) * M], ACT.Copy,
                        scale=xs[:, q, t, f:f + 1]).then_inc(mul_done, 1)

            turned_dense()
            act.wait_ge(w1_in, 16)
            nc.scalar.copy(w1_hi[:], w1).then_inc(w1_high, 1)
            act.wait_ge(ws_sum, 1)
            r = krows(ZB - 1)
            nc.scalar.copy(ws_hi[0:ROWS, 0:ZB - 1, :], ws[0:ROWS, 0:ZB - 1, :])
            nc.scalar.copy(ws_hi[0:r, ZB - 1, :], ws[0:r, ZB - 1, :]).then_inc(ws_high, 1)
            early_group_out()
            for piece in range(4):
                turn1_out(0, piece, y_ps[0:NF, piece, :])
            for k in range(ZB):
                z_high_out(0, k, k)
            c_high_out(0, 0)
            act.wait_ge(top_in, 96)

            def chunk(c, first=False, last=False):
                for q in range(GROUPS):
                    prep = not (last and q == GROUPS - 1)
                    g1 = c * GROUPS + q + 1
                    for s in range(SLOTS):
                        t, j = divmod(s, NBANK)
                        tile = c * TPC + q * TILES + t
                        if q == GROUPS - 1 and s == KEEP_Z1_SLOT:
                            keep_z1(c)
                        if KIND[j] == "A":
                            multiply(tile, q, t, j)
                        if j == 0 and not (first and q == 0 and t < 2):
                            gram_read(tile - 2, (q * BG + (t - 2) * BT) % P)
                        if prep:
                            if s == turn2_slot(first, q):
                                to = (c, q + 1) if q < 3 else (c + 1, 0)
                                turn2_out(*to, turn2_bank(to[1]))
                            piece = turn1_piece(first, q, s)
                            if piece is not None and not last:
                                turn1_out(c + 1, piece, t_ps[0:NF, turn1_bank(piece), :])
                            k, r = divmod(s - PRODUCT_SLOT - HIGH_LAG, STEP)
                            if r == 0 and 0 <= k < ZB:
                                z_high_out(g1, k, (q + 1) * ZB + k)
                            if s == C_SLOT:
                                c_high_out(g1, (q + 1) % 2)
                        if j == FINISH and not (first and q == 0 and t == 0):
                            cur2_high_out(tile - 1, (t + 1) % 2)
                        if not first:
                            if q == 0 and s == KEEP_Z2_SLOT:
                                keep_z2(c - 1)
                            if q == 0 and s == Z3_SLOT:
                                z3_out(c - 1)
                            if q == 0 and s == H1_SLOT:
                                h1_out(c - 1)
                            if q == 0 and s == H2_SLOT:
                                h2_out(c - 1)
                            if q == 1 and s == Y_SLOT:
                                y_read(c - 1)
                                send(c - 1)

            chunk(0, first=True)
            with act.Fori(1, NCHUNK - 1) as c:
                chunk(c)
            c = NCHUNK - 1
            chunk(c, last=True)
            gram_read(NCHUNK * TPC - 2, P - 2 * BT)
            cur2_high_out(NCHUNK * TPC - 1, 1)
            gram_read(NCHUNK * TPC - 1, P - BT)
            keep_z2(c)
            z3_out(c)
            h1_out(c, t_ps[:, 0, :])
            h2_out(c)
            y_read(c)
            send(c)

        @block.vector
        def _(dve):
            def embeddings_low(c, q, early=False):
                if early:
                    dve.wait_ge(early_out, 2)
                else:
                    dve.wait_ge(turned_out, turn2_count(c, q))
                nc.vector.tensor_tensor(xhl[:, q, :, 1, 0:NF], xs[:, q, :, :],
                                        xhl[:, q, :, 0, 0:NF].bitcast(F32),
                                        ALU.subtract).then_inc(x_low, 1)

            def products(c, q, k):
                i = q * ZB + k
                r = krows(k)
                start = isinstance(c, int) and c == 0 and q == 0
                if k == 0 and start:
                    dve.wait_ge(early_one, 16 * KB)
                elif k == 0:
                    dve.wait_ge(one_in[q % 2], 16 * KB * (c * (GROUPS // 2) + q // 2 + q % 2))
                if start and k in POOL_BLOCKS:
                    dve.wait_ge(early_other[k], 16 * loads(k))
                else:
                    dve.wait_ge(other_in[i % RING], other_count(c, i))
                wait(dve, z_low, c * BLOCKS + i - 1)
                nc.vector.tensor_tensor(zp[0:r, i % 2, :], one_side[0:r, q % 2, :],
                                        other_side[0:r, i % RING, :], ALU.mult).then_inc(multiplied, 1)

            def z_low_out(g, k, i):
                dve.wait_ge(z_high, g * ZB + k + 1)
                r = krows(k)
                nc.vector.tensor_tensor(z_lo[0:r, k % 3, :], zp[0:r, i % 2, :],
                                        z_hi[0:r, k % 3, :].bitcast(F32),
                                        ALU.subtract).then_inc(z_low, 1)

            def c_low_out(g, u):
                dve.wait_ge(c_high, g + 1)
                nc.vector.tensor_tensor(c_lo[:, u, :], c_ps[:], c_hi[:, u, :].bitcast(F32),
                                        ALU.subtract).then_inc(c_low, 1)

            def z1_out(g, q, kept):
                dve.wait_ge(l1_step, (g + 1) * ZB)
                wait(dve, z1_kept, kept)
                nc.vector.tensor_reduce(z1[:, q * BG:(q + 1) * BG],
                                        c_ps[:].rearrange("m (b d) -> m b d", d=D), AX_X,
                                        ALU.add).then_inc(z1_sum, 1)

            def accumulate(tile, q, t, j):
                dve.wait_ge(y_ready, tile * NBANK + j + 1)
                done = stt_count(0, j) - WIDTH[j]
                for i in range(WIDTH[j]):
                    n = done + i
                    f = FB * j + i
                    y = y_ps[:, (t * NBANK + j) % YB, i * M:(i + 1) * M]
                    to = part[:, t % 2, n % 2, :]
                    x = xs[:, q, t, f:f + 1]
                    if n < 2:
                        wait(dve, half_done, tile - 1)
                        nc.vector.tensor_scalar(to, y, x, None, ALU.mult).then_inc(stt_done, 1)
                    else:
                        dve.wait_ge(stt_done, tile * STT + n - 1)
                        nc.vector.scalar_tensor_tensor(out=to, in0=y, scalar=x, in1=to, op0=ALU.mult,
                                                       op1=ALU.add).then_inc(stt_done, 1)

            def finish(tile, u):
                dve.wait_ge(stt_done, (tile + 1) * STT)
                dve.wait_ge(add_done, (tile + 1) * ADDS)
                nc.vector.tensor_tensor(half[:, u, :, :], part[:, u, 0:2, :], part[:, u, 2:4, :],
                                        ALU.add).then_inc(half_done, 1)
                dve.wait_ge(half_done, tile + 1)
                wait(dve, gram_ready, tile - 1)
                nc.vector.tensor_tensor(cur2[:, u, :], half[:, u, 0, :], half[:, u, 1, :],
                                        ALU.add).then_inc(cur2_ready, 1)

            def cur2_low_out(tile, u):
                dve.wait_ge(cur2_high, tile + 1)
                nc.vector.tensor_tensor(cur2_lo[:, u, :], cur2[:, u, :], cur2_hi[:, u, :].bitcast(F32),
                                        ALU.subtract).then_inc(cur2_low, 1)

            nc.vector.memset(xd[:].bitcast(F32), 0.0).then_inc(xd_zero, 1)
            dve.wait_ge(w1_high, 1)
            nc.vector.tensor_tensor(w1_lo[:], w1, w1_hi[:].bitcast(F32), ALU.subtract).then_inc(w1_low, 1)
            dve.wait_ge(pairs_in, 16 * len(pair_list))
            r = krows(ZB - 1)
            nc.vector.tensor_tensor(ws[0:ROWS, 0:ZB - 1, :], wab[0:ROWS, 0, 0:ZB - 1, :],
                                    wab[0:ROWS, 1, 0:ZB - 1, :], ALU.add)
            nc.vector.tensor_tensor(ws[0:r, ZB - 1, :], wab[0:r, 0, ZB - 1, :], wab[0:r, 1, ZB - 1, :],
                                    ALU.add).then_inc(ws_sum, 1)
            dve.wait_ge(ws_high, 1)
            nc.vector.tensor_tensor(ws_lo[0:ROWS, 0:ZB - 1, :], ws[0:ROWS, 0:ZB - 1, :],
                                    ws_hi[0:ROWS, 0:ZB - 1, :].bitcast(F32), ALU.subtract)
            nc.vector.tensor_tensor(ws_lo[0:r, ZB - 1, :], ws[0:r, ZB - 1, :],
                                    ws_hi[0:r, ZB - 1, :].bitcast(F32), ALU.subtract).then_inc(ws_low, 1)
            embeddings_low(0, 0, early=True)
            products(0, 0, 0)
            for k in range(ZB):
                if k + 1 < ZB:
                    products(0, 0, k + 1)
                z_low_out(0, k, k)
            c_low_out(0, 0)

            def chunk(c, first=False, last=False):
                for q in range(GROUPS):
                    prep = not (last and q == GROUPS - 1)
                    g1 = c * GROUPS + q + 1
                    nxt = (c, q + 1) if q < 3 else (c + 1, 0)
                    for s in range(SLOTS):
                        t, j = divmod(s, NBANK)
                        tile = c * TPC + q * TILES + t
                        if KIND[j] == "D":
                            accumulate(tile, q, t, j)
                        if prep:
                            if s == PRODUCT_SLOT - 1:
                                embeddings_low(*nxt)
                            k, r = divmod(s - PRODUCT_SLOT, STEP)
                            if r == 0 and 0 <= k < ZB:
                                products(*nxt, k)
                            k, r = divmod(s - PRODUCT_SLOT - LOW_LAG, STEP)
                            if r == 0 and 0 <= k < ZB:
                                z_low_out(g1, k, (q + 1) * ZB + k)
                            if s == C_SLOT + 1:
                                c_low_out(g1, (q + 1) % 2)
                        if s == Z1_SLOT:
                            z1_out(c * GROUPS + q, q, c)
                        if j == FINISH and not (first and q == 0 and t == 0):
                            finish(tile - 1, (t + 1) % 2)
                        if j == FINISH_LOW and not (first and q == 0 and t == 0):
                            cur2_low_out(tile - 1, (t + 1) % 2)

            chunk(0, first=True)
            with dve.Fori(1, NCHUNK - 1) as c:
                chunk(c)
            chunk(NCHUNK - 1, last=True)
            finish(NCHUNK * TPC - 1, 1)
            cur2_low_out(NCHUNK * TPC - 1, 1)

        @block.tensor
        def _(pe):
            def turn_dense():
                pe.wait_ge(dense_in, 16)
                pe.wait_ge(ident_in, 16)
                for c in range(NCHUNK):
                    last = nc.tensor.transpose(t_ps[0:ND, 0, c * P:(c + 1) * P], dn[:, c, :], ident[:])
                last.then_inc(turned, 1)

            def turn1_waits(chunk, piece):
                if piece == 0:
                    pe.wait_ge(gathered, 16 * NF * (chunk + 1))
                pe.wait_ge(turned_out, turn1_count(chunk, piece) - 2)

            def turn2_waits(chunk, q):
                if q < 2:
                    pe.wait_ge(turned_out, turn1_count(chunk, 3))
                else:
                    pe.wait_ge(turned_out, turn2_count(chunk, q) - 2)

            def turn1(piece, to):
                for i in range(4):
                    d = 4 * piece + i
                    last = nc.tensor.transpose(to[:, i * P:(i + 1) * P], xg[:, :, d], ident[:])
                last.then_inc(turned, 1)

            def turn_early():
                pe.wait_ge(gathered, 16 * NF)
                for d in range(D):
                    last = nc.tensor.transpose(t_ps[0:NF, 1, d * BG:(d + 1) * BG], xg[0:BG, :, d],
                                               ident[0:BG, 0:BG])
                last.then_inc(early, 1)
                pe.wait_ge(turned_out, 1)
                pe.wait_ge(early_out, 1)
                turn2(0, 0, early)

            def turn2(q, bank, done=turned):
                for t in range(TILES):
                    a = (q * TILES + t) * P
                    last = nc.tensor.transpose(t_ps[:, bank, t * NF:(t + 1) * NF], xt[0:NF, a:a + P],
                                               ident[0:NF, 0:NF])
                last.then_inc(done, 1)

            def layer1(g, k):
                if k == 0:
                    wait(pe, z1_sum, g)
                    wait(pe, c_low, g)
                pe.wait_ge(z_high, g * ZB + k + 1)
                r = krows(k)
                hi, lo = z_hi[0:r, k % 3, :], z_lo[0:r, k % 3, :]
                nc.tensor.matmul(c_ps[:], ws_hi[0:r, k, :], hi, start=(k == 0), stop=False)
                nc.tensor.matmul(c_ps[:], ws_lo[0:r, k, :], hi, start=False, stop=False)
                pe.wait_ge(z_low, g * ZB + k + 1)
                nc.tensor.matmul(c_ps[:], ws_hi[0:r, k, :], lo, start=False,
                                 stop=(k == ZB - 1)).then_inc(l1_step, 1)

            def layer2(tile, q, t, j, g, others=lambda: None):
                u = q % 2
                if t == 0 and j == 0:
                    pe.wait_ge(c_high, g)
                    pe.wait_ge(c_low, g)
                pj, pt = j - YB, tile
                if pj < 0:
                    pj, pt = pj + NBANK, tile - 1
                if isinstance(tile, int) and tile == 0 and j < YB:
                    pe.wait_ge(turned_out, turn1_count(0, j))
                elif KIND[pj] == "D":
                    wait(pe, stt_done, stt_count(pt, pj))
                else:
                    wait(pe, mul_done, mul_count(pt, pj))
                n = WIDTH[j] * M
                w = slice(FB * j * M, FB * j * M + n)
                to = y_ps[:, (t * NBANK + j) % YB, 0:n]
                hi = c_hi[:, u, t * P:(t + 1) * P]
                lo = c_lo[:, u, t * P:(t + 1) * P]
                nc.tensor.matmul(to, hi, w1_hi[:, w], start=True, stop=False)
                nc.tensor.matmul(to, hi, w1_lo[:, w], start=False, stop=False)
                others()
                nc.tensor.matmul(to, lo, w1_hi[:, w], start=False, stop=True).then_inc(y_ready, 1)

            def gram(tile, groups, n, tails):
                wait(pe, gram_out, tile)
                if tails is not None:
                    pe.wait_ge(tail_out, tails)
                pe.wait_ge(xd_ready[n // HALF % 2], 16 * BT * groups)
                pe.wait_ge(cur2_high, tile + 1)
                to = m_ps[:, 0:BT * (NF + 1)].rearrange("p (b f) -> p b f", f=NF + 1)
                u = n % 2
                x_hi, x_lo = (xd[:, n // HALF % 2, n % HALF, :, i, :] for i in range(2))
                nc.tensor.matmul(to, cur2_hi[:, u, :], x_hi, start=True, stop=False)
                nc.tensor.matmul(to, cur2_hi[:, u, :], x_lo, start=False, stop=False)
                pe.wait_ge(cur2_low, tile + 1)
                nc.tensor.matmul(to, cur2_lo[:, u, :], x_hi, start=False, stop=True
                                 ).then_inc(gram_ready, 1)

            def layer3(c, lo, hi):
                if lo == 0:
                    pe.wait_ge(gram_out, TPC * (c + 1))
                for f in range(lo, min(hi, NF)):
                    last = nc.tensor.matmul(m_ps[:, 0:P], w2[:, f, :], gs[:, f, :], start=(f == 0),
                                            stop=(f == NF - 1))
                if hi >= NF:
                    last.then_inc(tail_ready, 1)

            def tower1(c, grams, n):
                if n == 0:
                    pe.wait_ge(gram_out, grams)
                    pe.wait_ge(tail_out, 4 * c + 1)
                    pe.wait_ge(z1_kept, c + 1)
                    pe.wait_ge(z2_kept, c + 1)
                to = m_ps[:, n * P:(n + 1) * P]
                w = slice(n * P, (n + 1) * P)
                for k, z in enumerate((z1m, z2m, z3m)):
                    nc.tensor.matmul(to, wt1[:, k, w], z[:], start=(n == 0 and k == 0), stop=False,
                                     skip_group_check=True)
                d = bass.ds(c * P, P)
                last = nc.tensor.matmul(to, wt1d[:, w], dnt[:, d], start=False, stop=(n == N1 - 1),
                                        skip_group_check=True)
                if n == N1 - 1:
                    last.then_inc(tail_ready, 1)

            def last_tower1(c, parts, first=False, done=False):
                to = t_ps[:, 0, :].rearrange("m (n b) -> m n b", b=P)
                for n in range(N1):
                    w = slice(n * P, (n + 1) * P)
                    for weights, z in parts:
                        last = nc.tensor.matmul(to[:, n, :], weights[:, w], z,
                                                start=(first and n == 0 and z is parts[0][1]),
                                                stop=(done and n == N1 - 1), skip_group_check=True)
                if done:
                    last.then_inc(tail_ready, 1)

            def tower2(c, grams, n):
                if n == 0:
                    pe.wait_ge(gram_out, grams)
                    pe.wait_ge(tail_out, 4 * c + 2)
                for k in range(N1):
                    last = nc.tensor.matmul(m_ps[:, n * P:(n + 1) * P], wt2[:, k, n * P:(n + 1) * P],
                                            h1s[:, k, :], start=(n == 0 and k == 0),
                                            stop=(n == N2 - 1 and k == N1 - 1), skip_group_check=True)
                if n == N2 - 1:
                    last.then_inc(tail_ready, 1)

            def tower3(c, grams):
                pe.wait_ge(gram_out, grams)
                pe.wait_ge(tail_out, 4 * c + 3)
                for k in range(N2):
                    last = nc.tensor.matmul(m_ps[0:1, 0:P], wt3[:, k:k + 1], h2s[:, k, :],
                                            start=(k == 0), stop=(k == N2 - 1))
                last.then_inc(tail_ready, 1)

            turn_dense()
            turn_early()
            pe.wait_ge(ws_low, 1)
            for piece in range(4):
                turn1(piece, y_ps[0:NF, piece, :])
            for k in range(ZB):
                layer1(0, k)
            pe.wait_ge(w1_low, 1)
            pe.wait_ge(top_in, 96)
            pe.wait_ge(w2_in, 16)

            def chunk(c, first=False, last=False):
                for q in range(GROUPS):
                    prep = not (last and q == GROUPS - 1)
                    g1 = c * GROUPS + q + 1
                    for s in range(SLOTS):
                        t, j = divmod(s, NBANK)
                        tile = c * TPC + q * TILES + t

                        piece = turn1_piece(first, q, s)

                        def others():
                            if prep and s == turn2_slot(first, q):
                                turn2_waits(*((c, q + 1) if q < 3 else (c + 1, 0)))
                            if piece is not None and not last:
                                turn1_waits(c + 1, piece)

                        layer2(tile, q, t, j, g1, others)
                        if prep:
                            if s == turn2_slot(first, q):
                                turn2((q + 1) % GROUPS, turn2_bank((q + 1) % GROUPS))
                            if piece is not None and not last:
                                turn1(piece, t_ps[0:NF, turn1_bank(piece), :])
                            k, r = divmod(s - PRODUCT_SLOT - L1_LAG, STEP)
                            if r == 0 and 0 <= k < ZB:
                                layer1(g1, k)
                        if j == GRAM and not (first and q == 0 and t == 0):
                            between = not first and 1 <= q * TILES + t <= 4
                            n = q * TILES + t - 1
                            gram(tile - 1, c * GROUPS + n // TILES + 1, n % TPC,
                                 4 * (c - 1) + n + 1 if between else None)
                        if not first:
                            if q == 0 and L3_SLOT <= s < L3_SLOT - (-NF // L3_STEP):
                                layer3(c - 1, L3_STEP * (s - L3_SLOT), L3_STEP * (s - L3_SLOT + 1))
                            if q == 0 and TOWER1_SLOT <= s < TOWER1_SLOT + N1:
                                tower1(c - 1, TPC * c + 1, s - TOWER1_SLOT)
                            if q == 0 and TOWER2_SLOT <= s < TOWER2_SLOT + N2:
                                tower2(c - 1, TPC * c + 2, s - TOWER2_SLOT)
                            if q == 1 and s == TOWER3_SLOT:
                                tower3(c - 1, TPC * c + 3)

            chunk(0, first=True)
            with pe.Fori(1, NCHUNK - 1) as c:
                chunk(c)
            c = NCHUNK - 1
            chunk(c, last=True)
            n = NCHUNK * TPC
            pe.wait_ge(z1_kept, NCHUNK)
            pe.wait_ge(turned_out, turn2_count(c, GROUPS - 1))
            last_tower1(c, ((wt1[:, 0, :], z1m[:]), (wt1d[:], dnt[:, c * P:])), first=True)
            gram(n - 1, n // TILES, TPC - 1, None)
            layer3(c, 0, NF)
            pe.wait_ge(z2_kept, NCHUNK)
            last_tower1(c, ((wt1[:, 1, :], z2m[:]),))
            pe.wait_ge(tail_out, 4 * c + 1)
            last_tower1(c, ((wt1[:, 2, :], z3m[:]),), done=True)
            for i in range(N2):
                tower2(c, n, i)
            tower3(c, n)


def kernel(**inputs):
    import numpy as _np
    import concourse.bacc as _bacc
    from concourse import mybir as _mybir
    from concourse.bass_utils import run_bass_kernel_spmd as _run

    nc = _bacc.Bacc("TRN2", target_bir_lowering=False, num_devices=1)
    arrays = {}

    def given(name, a):
        a = _np.ascontiguousarray(a)
        arrays[f"in_{name}_dram"] = a
        return nc.dram_tensor(f"in_{name}_dram", a.shape, _mybir.dt.from_np(a.dtype), kind="ExternalInput").ap()

    identity = _np.eye(P, dtype=_np.float32)

    args = [given(n, inputs[n]) for n in ("dense_ctx", "ids")]
    args.append([given(f"tbl_{f}", inputs[f"tbl_{f}"]) for f in range(NF)])
    args += [given("W_top1", inputs["W_top1"]),
             given("b_top1", _np.asarray(inputs["b_top1"]).reshape(N1, P).T),
             given("W_top2", inputs["W_top2"]),
             given("b_top2", _np.asarray(inputs["b_top2"]).reshape(N2, P).T),
             given("W_top3", _np.asarray(inputs["W_top3"]).reshape(N2, P).T)]
    args += [given(n, inputs[n]) for n in ("L0_rec_f0", "L0_rec_f1", "L0_rec_f2")]
    args += [given("identity", identity)]
    out = nc.dram_tensor("out_0_dram", (NB, 1), _mybir.dt.float32, kind="ExternalOutput").ap()
    build(nc, *args, out)
    r = _run(nc, [arrays], core_ids=[0])
    return r.results[0]["out_0_dram"]
```
